# Optimizing a Trainium2 kernel written in Bass

```python
import numpy as np
import jax
import jax.numpy as jnp

def _softmax(x, axis=-1):
    return jax.nn.softmax(x, axis=axis)

def _gelu(x):
    return jax.nn.gelu(x, approximate=True)

def _silu(x):
    return jax.nn.silu(x)

def _sigmoid(x):
    return jax.nn.sigmoid(x)

def _layernorm(x, axis=-1, eps=1e-05):
    m = jnp.mean(x, axis=axis, keepdims=True)
    v = jnp.var(x, axis=axis, keepdims=True)
    return (x - m) / jnp.sqrt(v + eps)

def _scatter_add(tgt, idx, src, axis=0):
    return tgt.at[idx].add(src)

def _segment_sum(src, seg, n):
    return jax.ops.segment_sum(src, seg, n)
kernel_name = 'mk_flamingo_gated_d2_seqx_r4_66d0e7'

def setup_inputs(seed: int=0):
    np.random.seed(seed)
    _w = jnp.asarray

    def _rec_inputs():
        import jax
        import jax.numpy as jnp
        _rk = jax.random.key(seed)
        x = -0.0003929 + 0.9999 * jax.random.normal(jax.random.fold_in(_rk, 1), (16, 128, 1024), jnp.float32)
        _lenS = 128 - jax.random.randint(jax.random.fold_in(_rk, 7), (16,), 0, max(1, 128 // 4) + 1, jnp.int32)
        _lenS2 = 128 - jax.random.randint(jax.random.fold_in(_rk, 8), (16,), 0, max(1, 128 // 4) + 1, jnp.int32)
        _ctx_4096P = jax.random.normal(jax.random.fold_in(_rk, 11), (16, 16, 1024), jnp.float32)
        _ctx_4096c = jax.random.dirichlet(jax.random.fold_in(_rk, 511), 0.3 * jnp.ones((16,), jnp.float32), (16, 128))
        _ctx_4096t = jnp.einsum('bsk,bkd->bsd', _ctx_4096c, _ctx_4096P)
        _ctx_4096t = _ctx_4096t * jax.lax.rsqrt(jnp.mean(jnp.square(_ctx_4096t)) + 1e-12) * 0.953939
        ctx_4096 = 2.81802e-05 + 1.00001 * (_ctx_4096t + 0.3 * jax.random.normal(jax.random.fold_in(_rk, 611), (16, 128, 1024), jnp.float32))
        _validS = jnp.arange(128)[None, :] < _lenS[:, None]
        _validS2 = jnp.arange(128)[None, :] < _lenS2[:, None]
        _causal = jnp.tril(jnp.ones((128, 128), dtype=bool))
        mask_1x1xSxS2_bk0 = jnp.logical_not(jnp.broadcast_to(_validS2[0:1, None, None, :], (1, 1, 128, 128)))
        _g = jax.random.normal(jax.random.fold_in(_rk, 9001), (2, 2), jnp.float32)
        _g = jnp.sign(_g) * jnp.maximum(jnp.abs(_g), 1.0) + (_g == 0) * 1.0
        g_xattn = _g[0]
        g_ffn = _g[1]
        return (x, ctx_4096, mask_1x1xSxS2_bk0, g_xattn, g_ffn)
    x, ctx_4096, mask_1x1xSxS2_bk0, g_xattn, g_ffn = _rec_inputs()

    def _L0_xattn_setup():
        import jax, jax.numpy as jnp
        import numpy as np
        DIM = 128
        HEADS = 8
        DIM_HEAD = 64
        HIDDEN = HEADS * DIM_HEAD
        SCALE = DIM_HEAD ** (-0.5)
        key = jax.random.key(seed)
        ks = jax.random.split(key, 9)
        b, n = (8, 1024)
        std = 1.0 / np.sqrt(DIM)
        return {'q': jax.random.normal(ks[0], (b, DIM, n), jnp.float32), 'k': jax.random.normal(ks[1], (b, DIM, n), jnp.float32), 'v': jax.random.normal(ks[2], (b, DIM, n), jnp.float32), 'Wq': jax.random.normal(ks[3], (HIDDEN, DIM), jnp.float32) * std, 'Wk': jax.random.normal(ks[4], (HIDDEN, DIM), jnp.float32) * std, 'Wv': jax.random.normal(ks[5], (HIDDEN, DIM), jnp.float32) * std, 'Wo': jax.random.normal(ks[6], (DIM, HIDDEN), jnp.float32) * (1.0 / np.sqrt(HIDDEN)), 'bo': jax.random.normal(ks[7], (DIM,), jnp.float32) * 0.01, 'g': jnp.ones((1, DIM, 1), jnp.float32)}
    _L0_xattn_all = _L0_xattn_setup()
    _L0_xattn_in = {k: v for k, v in _L0_xattn_all.items() if k in ('Wq', 'Wk', 'Wv', 'Wo', 'bo', 'g')}
    del _L0_xattn_all

    def _L0_ffn_setup():
        import jax, jax.numpy as jnp
        import numpy as np
        E = 8
        R = 16
        TOP_K = 2
        SCALING = 32.0 / 16.0
        D_IN = 1024
        D_OUT = 1024
        key = jax.random.key(seed)
        ks = jax.random.split(key, 6)
        x = jax.random.normal(ks[0], (4, 512, D_IN), jnp.float32)
        Wb = jax.random.normal(ks[1], (D_OUT, D_IN), jnp.float32) * 0.02
        bias = jax.random.normal(ks[2], (D_OUT,), jnp.float32) * 0.02
        Wr = jax.random.normal(ks[3], (E, D_IN), jnp.float32) * 0.01
        A = jax.random.normal(ks[4], (E, R, D_IN), jnp.float32) * (1.0 / np.sqrt(D_IN))
        Bm = jax.random.normal(ks[5], (E, D_OUT, R), jnp.float32) * 0.01
        return {'x': x, 'Wb': Wb, 'bias': bias, 'Wr': Wr, 'A': A, 'Bm': Bm}
    _L0_ffn_all = _L0_ffn_setup()
    _L0_ffn_in = {k: v for k, v in _L0_ffn_all.items() if k in ('Wb', 'bias', 'Wr', 'A', 'Bm')}
    del _L0_ffn_all

    def _L1_xattn_setup():
        import jax, jax.numpy as jnp
        import numpy as np
        B, T, D_MODEL = (1, 512, 1024)
        NUM_Q_HEADS, NUM_KV_HEADS, KEY_SIZE = (32, 8, 128)
        ATTN_MULT = 0.08838834764831845
        MAX_ATTN_VAL = 30.0

        def rotate_half(x):
            x1, x2 = jnp.split(x, 2, axis=-1)
            return jnp.concatenate((-x2, x1), axis=-1)

        def apply_rope(x):
            b, t, h, d = x.shape
            exponents = jnp.arange(0, d, 2, dtype=jnp.float32)
            inv_freq = 1.0 / 10000.0 ** (exponents / d)
            pos = jnp.arange(t, dtype=jnp.float32)
            phase = pos[:, None] * inv_freq[None, :]
            phase = jnp.tile(phase, (1, 2))[None, :, None, :]
            return (x * jnp.cos(phase) + rotate_half(x) * jnp.sin(phase)).astype(x.dtype)
        key = jax.random.key(seed)
        ks = jax.random.split(key, 8)
        query = jax.random.normal(ks[0], (B, T, D_MODEL), dtype=jnp.float32)
        kk = jax.random.normal(ks[1], (B, T, D_MODEL), dtype=jnp.float32)
        vv = jax.random.normal(ks[2], (B, T, D_MODEL), dtype=jnp.float32)
        mask = jnp.tril(jnp.ones((T, T), dtype=bool))[None, None, :, :]
        s = 0.02
        Wq = jax.random.normal(ks[3], (D_MODEL, NUM_Q_HEADS * KEY_SIZE), dtype=jnp.float32) * s
        Wk = jax.random.normal(ks[4], (D_MODEL, NUM_KV_HEADS * KEY_SIZE), dtype=jnp.float32) * s
        Wv = jax.random.normal(ks[5], (D_MODEL, NUM_KV_HEADS * KEY_SIZE), dtype=jnp.float32) * s
        Wo = jax.random.normal(ks[6], (NUM_Q_HEADS * KEY_SIZE, D_MODEL), dtype=jnp.float32) * s
        return {'query': query, 'key': kk, 'value': vv, 'mask': mask, 'Wq': Wq, 'Wk': Wk, 'Wv': Wv, 'Wo': Wo}
    _L1_xattn_all = _L1_xattn_setup()
    _L1_xattn_in = {k: v for k, v in _L1_xattn_all.items() if k in ('Wq', 'Wk', 'Wv', 'Wo')}
    del _L1_xattn_all

    def _L1_ffn_setup():
        import jax, jax.numpy as jnp
        import numpy as np

        @jax.custom_vjp
        def ste_sign(w):
            return jnp.sign(w)

        def _ste_fwd(w):
            return (jnp.sign(w), w)

        def _ste_bwd(w, g):
            mask = ((w > -1) & (w < 1)).astype(g.dtype)
            return (g * mask,)
        ste_sign.defvjp(_ste_fwd, _ste_bwd)
        key = jax.random.key(seed)
        k = jax.random.split(key, 6)
        B, S, H, O, E = (4, 512, 1024, 1024, 8)
        return {'x': jax.random.normal(k[0], (B, S, H), dtype=jnp.float32), 'weight': jax.random.normal(k[1], (O, H), dtype=jnp.float32) * 0.02, 'bias': jax.random.normal(k[2], (O,), dtype=jnp.float32) * 0.02, 'gate_w': jax.random.normal(k[3], (E, H), dtype=jnp.float32) * 0.02, 'in_channel_scale': jax.random.normal(k[4], (E, H), dtype=jnp.float32), 'out_channel_scale': jax.random.normal(k[5], (E, O), dtype=jnp.float32)}
    _L1_ffn_all = _L1_ffn_setup()
    _L1_ffn_in = {k: v for k, v in _L1_ffn_all.items() if k in ('weight', 'bias', 'gate_w', 'in_channel_scale', 'out_channel_scale')}
    del _L1_ffn_all
    return {'x': x, 'ctx_4096': ctx_4096, 'mask_1x1xSxS2_bk0': mask_1x1xSxS2_bk0, 'g_xattn': g_xattn, 'g_ffn': g_ffn, 'L0_xattn_Wq': _L0_xattn_in['Wq'], 'L0_xattn_Wk': _L0_xattn_in['Wk'], 'L0_xattn_Wv': _L0_xattn_in['Wv'], 'L0_xattn_Wo': _L0_xattn_in['Wo'], 'L0_xattn_bo': _L0_xattn_in['bo'], 'L0_xattn_g': _L0_xattn_in['g'], 'L0_ffn_Wb': _L0_ffn_in['Wb'], 'L0_ffn_bias': _L0_ffn_in['bias'], 'L0_ffn_Wr': _L0_ffn_in['Wr'], 'L0_ffn_A': _L0_ffn_in['A'], 'L0_ffn_Bm': _L0_ffn_in['Bm'], 'L1_xattn_Wq': _L1_xattn_in['Wq'], 'L1_xattn_Wk': _L1_xattn_in['Wk'], 'L1_xattn_Wv': _L1_xattn_in['Wv'], 'L1_xattn_Wo': _L1_xattn_in['Wo'], 'L1_ffn_weight': _L1_ffn_in['weight'], 'L1_ffn_bias': _L1_ffn_in['bias'], 'L1_ffn_gate_w': _L1_ffn_in['gate_w'], 'L1_ffn_in_channel_scale': _L1_ffn_in['in_channel_scale'], 'L1_ffn_out_channel_scale': _L1_ffn_in['out_channel_scale']}

def reference(x, ctx_4096, mask_1x1xSxS2_bk0, g_xattn, g_ffn, L0_xattn_Wq, L0_xattn_Wk, L0_xattn_Wv, L0_xattn_Wo, L0_xattn_bo, L0_xattn_g, L0_ffn_Wb, L0_ffn_bias, L0_ffn_Wr, L0_ffn_A, L0_ffn_Bm, L1_xattn_Wq, L1_xattn_Wk, L1_xattn_Wv, L1_xattn_Wo, L1_ffn_weight, L1_ffn_bias, L1_ffn_gate_w, L1_ffn_in_channel_scale, L1_ffn_out_channel_scale):
    import jax
    import jax.numpy as jnp

    def _L0_xattn_ref(q, k, v, Wq, Wk, Wv, Wo, bo, g):
        import jax, jax.numpy as jnp
        import numpy as np
        DIM = 128
        HEADS = 8
        DIM_HEAD = 64
        HIDDEN = HEADS * DIM_HEAD
        SCALE = DIM_HEAD ** (-0.5)
        b = q.shape[0]
        qh = jnp.einsum('bcn,oc->bon', q, Wq).reshape(b, HEADS, DIM_HEAD, -1)
        kh = jnp.einsum('bcn,oc->bon', k, Wk).reshape(b, HEADS, DIM_HEAD, -1)
        vh = jnp.einsum('bcn,oc->bon', v, Wv).reshape(b, HEADS, DIM_HEAD, -1)
        qh = jax.nn.softmax(qh, axis=-2) * SCALE
        kh = jax.nn.softmax(kh, axis=-1)
        context = jnp.einsum('bhdn,bhen->bhde', kh, vh)
        out = jnp.einsum('bhde,bhdn->bhen', context, qh)
        out = out.reshape(b, HIDDEN, -1)
        out = jnp.einsum('bcn,oc->bon', out, Wo) + bo[None, :, None]
        norm = jnp.maximum(jnp.sqrt(jnp.sum(out * out, axis=1, keepdims=True)), 1e-12)
        return out / norm * g * np.sqrt(DIM)

    def _L0_ffn_ref(x, Wb, bias, Wr, A, Bm):
        import jax, jax.numpy as jnp
        import numpy as np
        E = 8
        R = 16
        TOP_K = 2
        SCALING = 32.0 / 16.0
        D_IN = 1024
        D_OUT = 1024
        xf = x.reshape(-1, x.shape[-1])
        T = xf.shape[0]
        logits = xf @ Wr.T
        probs = jax.nn.softmax(logits, axis=-1)
        topk_p, topk_i = jax.lax.top_k(probs, TOP_K)
        topk_p = topk_p / jnp.sum(topk_p, axis=-1, keepdims=True)
        w = jnp.zeros((T, E), xf.dtype).at[jnp.arange(T)[:, None], topk_i].add(topk_p)
        h = jnp.einsum('ti,eri->ter', xf, A)
        lora = jnp.einsum('ter,te,eor->to', h, w, Bm) * SCALING
        base = xf @ Wb.T + bias
        out = (base + lora).reshape(*x.shape[:-1], D_OUT)
        return out

    def _L1_xattn_ref(query, key, value, mask, Wq, Wk, Wv, Wo):
        import jax, jax.numpy as jnp
        import numpy as np
        B, T, D_MODEL = (1, 512, 1024)
        NUM_Q_HEADS, NUM_KV_HEADS, KEY_SIZE = (32, 8, 128)
        ATTN_MULT = 0.08838834764831845
        MAX_ATTN_VAL = 30.0

        def rotate_half(x):
            x1, x2 = jnp.split(x, 2, axis=-1)
            return jnp.concatenate((-x2, x1), axis=-1)

        def apply_rope(x):
            b, t, h, d = x.shape
            exponents = jnp.arange(0, d, 2, dtype=jnp.float32)
            inv_freq = 1.0 / 10000.0 ** (exponents / d)
            pos = jnp.arange(t, dtype=jnp.float32)
            phase = pos[:, None] * inv_freq[None, :]
            phase = jnp.tile(phase, (1, 2))[None, :, None, :]
            return (x * jnp.cos(phase) + rotate_half(x) * jnp.sin(phase)).astype(x.dtype)
        b, t, _ = query.shape
        d = KEY_SIZE
        h, kv_h = (NUM_Q_HEADS, NUM_KV_HEADS)
        g = h // kv_h
        q = (query @ Wq).reshape(b, t, h, d)
        k = (key @ Wk).reshape(b, t, kv_h, d)
        v = (value @ Wv).reshape(b, t, kv_h, d)
        q = apply_rope(q)
        k = apply_rope(k)
        q = q.reshape(b, t, kv_h, g, d)
        logits = jnp.einsum('btkgd,bTkd->bkgtT', q, k).astype(jnp.float32)
        logits = logits * ATTN_MULT
        logits = MAX_ATTN_VAL * jnp.tanh(logits / MAX_ATTN_VAL)
        m = mask[:, :, None, :, :]
        logits = jnp.where(m, logits, -1e+30)
        weights = jax.nn.softmax(logits, axis=-1).astype(query.dtype)
        attn = jnp.einsum('bkgtT,bTkd->btkgd', weights, v)
        attn = attn.reshape(b, t, h * d)
        return attn @ Wo

    def _L1_ffn_ref(x, weight, bias, gate_w, in_channel_scale, out_channel_scale):
        import jax, jax.numpy as jnp
        import numpy as np

        @jax.custom_vjp
        def ste_sign(w):
            return jnp.sign(w)

        def _ste_fwd(w):
            return (jnp.sign(w), w)

        def _ste_bwd(w, g):
            mask = ((w > -1) & (w < 1)).astype(g.dtype)
            return (g * mask,)
        ste_sign.defvjp(_ste_fwd, _ste_bwd)
        B, S, H = x.shape
        xf = x.reshape(-1, H)
        router_logits = xf @ gate_w.T
        routing = jax.nn.softmax(router_logits.astype(jnp.float32), axis=1).astype(x.dtype)
        in_scale = routing @ in_channel_scale
        out_scale = routing @ out_channel_scale
        wb = ste_sign(weight)
        out = xf * in_scale @ wb.T * out_scale + bias
        return out.reshape(B, S, -1)
    x = x + jnp.tanh(g_xattn[0]) * _L0_xattn_ref(_layernorm(x, axis=-1), ctx_4096, ctx_4096, L0_xattn_Wq, L0_xattn_Wk, L0_xattn_Wv, L0_xattn_Wo, L0_xattn_bo, L0_xattn_g)
    x = x + jnp.tanh(g_ffn[0]) * _L0_ffn_ref(_layernorm(x, axis=-1), L0_ffn_Wb, L0_ffn_bias, L0_ffn_Wr, L0_ffn_A, L0_ffn_Bm)
    x = x + jnp.tanh(g_xattn[1]) * _L1_xattn_ref(_layernorm(x, axis=-1), ctx_4096, ctx_4096, mask_1x1xSxS2_bk0, L1_xattn_Wq, L1_xattn_Wk, L1_xattn_Wv, L1_xattn_Wo)
    x = x + jnp.tanh(g_ffn[1]) * _L1_ffn_ref(_layernorm(x, axis=-1), L1_ffn_weight, L1_ffn_bias, L1_ffn_gate_w, L1_ffn_in_channel_scale, L1_ffn_out_channel_scale)
    return x

_drawn_inputs = setup_inputs


def setup_inputs(seed=0):
    import zlib

    import numpy as np

    out = dict(_drawn_inputs(seed))
    spreads = {'g_ffn': (-1.0, 0.2), 'L0_xattn_g': (1.0, 0.2)}
    factors = {'L0_ffn_bias': 3.999, 'L1_ffn_bias': 8.0}
    for name, (base, spread) in spreads.items():
        noise = np.random.default_rng([zlib.crc32(name.encode()), seed]).standard_normal(out[name].shape)
        drawn = base * np.exp(spread * noise) if base else spread * noise
        out[name] = jnp.asarray(drawn.astype(out[name].dtype))
    for name, factor in factors.items():
        out[name] = (out[name] * factor).astype(out[name].dtype)
    return out
```

```python
from contextlib import ExitStack
import math

import numpy as np
import concourse.bass as bass
from concourse import mybir

F32 = mybir.dt.float32
F32R = mybir.dt.float32r
U8 = mybir.dt.uint8
U32 = mybir.dt.uint32
ALU = mybir.AluOpType
ACT = mybir.ActivationFunctionType
AX = mybir.AxisListType

P = 128
BANK = 512
BATCH, SEQ, DM = 16, 128, 1024
KT = DM // P
EPS = 1e-5
SPLIT = (("hi", "hi"), ("hi", "lo"), ("lo", "hi"))


def linear_attention_moe_stage(nc, x_in, c_in, WqT, WkT, Wv, WoT, bo, g_norm, gate_x, gate_f, WbT, bias, AT, WrT,
                               BmT, prio, x_out, xnT_out, ctxT_out):
    H, DH = 8, 64
    HID = H * DH
    MT = HID // P
    NE, R = 8, 16
    ER = NE * R

    with ExitStack() as ctx:
        def sb(name, shape, dt=F32):
            return ctx.enter_context(nc.sbuf_tensor("a_" + name, shape, dt))

        def ps(name, cols):
            return ctx.enter_context(nc.psum_tensor("ap_" + name, [P, cols], F32))

        def sem(name):
            return ctx.enter_context(nc.semaphore("a_" + name))

        def pair(name, shape):
            return {h: sb(f"{name}_{h}", shape, F32R) for h in ("hi", "lo")}

        wq, wk = pair("wq", [P, HID]), pair("wk", [P, HID])
        wb = pair("wb", [P, KT, DM])
        avo = sb("avo", [P, H, P])
        ar = sb("ar", [P, KT, ER + NE])
        bm = sb("bm", [ER, DM])
        ident, ones = sb("ident", [P, P]), sb("ones", [P, P])
        prio_sb = sb("prio", [P, NE])
        half_neg = sb("half_neg", [P, KT])
        eps = sb("eps", [P, 1])
        bo_sb, sc, tgf = sb("bo", [P, 1]), sb("sc", [P, 1]), sb("tgf", [P, 1])
        tgx, gn = sb("tgx", [P, 1]), sb("gn", [P, 1])
        tgb = sb("tgb", [P, DM])
        x_sb = [sb(f"xin{i}", [P, DM]) for i in range(2)]
        c_sb = [sb(f"c{i}", [P, DM]) for i in range(2)]
        xn_f = sb("xn_f", [P, DM])
        xn, cc = pair("xn", [P, DM]), pair("cc", [P, DM])
        cT = sb("cT", [P, KT, P])
        ke = sb("ke", [P, MT, DM])
        kneg, ksum, krec = sb("kneg", [P, MT]), sb("ksum", [P, MT]), sb("krec", [P, MT])
        qs = [sb(f"qs{i}", [P, HID]) for i in range(4)]
        qmax, qsum = sb("qmax", [P, H]), sb("qsum", [P, H])
        qrec = [sb(f"qrec{i}", [P, H]) for i in range(2)]
        qT = sb("qT", [P, MT, DM])
        keT, g_sb = qs[1:3], qs[0]
        w2 = sb("w2", [P, MT, P])
        o_sb = sb("o_sb", [P, DM])
        ss, rn = sb("ss", [P, KT]), sb("rn", [P, KT])
        t_sb = sb("t_sb", [P, DM])
        x1, x1b = sb("x1", [P, DM]), sb("x1b", [P, DM])
        sq = x1
        hT = sb("hT", [ER, P])
        xT_f = xn_f[:, :].rearrange("p (k t) -> p k t", k=KT)
        xT = pair("xT", [P, KT, P])
        h_sb = sb("h_sb", [P, ER])
        ex, rt, sel, tmp = (sb(n, [P, NE]) for n in ("ex", "rt", "sel", "tmp"))
        sm = sb("sm", [P, 8])
        x2 = sb("x2", [P, DM])
        x2T = sb("x2T", [P, KT, P])
        diag = x2T
        ln = {n: (sb(f"st_{n}", [P, 2, 6]), sb(f"mv_{n}", [P, 2]), sb(f"rs_{n}", [P, 1])) for n in ("x", "1", "2")}
        raw = [t_sb, x1, x1b, x2]

        p_k = ps("k", DM)
        p_tr = [ps("t0", BANK), ps("t1", BANK)]
        p_q = ps("q", BANK)
        p_y = ps("y", DM)
        p_g = ps("g", BANK)

        names = """norm_steps k_used const_in const_pool gates sc_done tgb_done w_hi w_lo avo_done avo_out
            cc_hi cc_lo xn_hi xn_lo tr_done tr_out k_proj kmax_done kexp krec_done q_proj qmax_done qsub qexp
            qsum_done qrec_done qnorm g_out w2_done w2_out out_done o_out sq_done
            ss_done ss_out ss_pow diag_done spread_done t_done x1_done x1b_done xT_hi xT_lo lora_done
            route_max route_exp route_step rt_done h_done h_turned hT_out y_done x2_done ctxT_st xnT_st x2_st"""
        S = {n: sem(n) for n in names.split()}
        w_land = [sem(f"w_land{i}") for i in range(4)]
        x_land = [sem(f"x_land{i}") for i in range(2)]
        c_land = [sem(f"c_land{i}") for i in range(2)]
        LN = {n: {k: sem(f"ln_{n}_{k}") for k in ("stats", "mv", "var", "rstd", "done")} for n in ("x", "1", "2")}

        ATT_UNITS = [("ctx", 0), ("ctx", 1)] + [("q", r) for r in range(KT)] + [("k", r) for r in range(KT)]
        FULL_UNITS = ([("ctx", 0), ("ctx", 1), ("q", 0), ("q", 1), ("q", 2), ("x", 0), ("x", 1)]
                      + [("q", r) for r in range(3, KT)] + [("k", r) for r in range(6)]
                      + [("n", 0), ("n", 1), ("k", 6), ("k", 7)])
        FFN_UNITS = [("x", 0), ("x", 1), ("n", 0), ("n", 1)]
        W_CHUNKS = KT + 2

        class Step:

            def __init__(self, s0, c, att, ffn, half):
                self.s, self.c, self.att, self.ffn = s0 + c, c, att, ffn
                self.par, self.half = c % 2, half
                self.units = FULL_UNITS if att and ffn else ATT_UNITS if att else FFN_UNITS
                self.tr0 = (s0 + (c - 1)) * len(FULL_UNITS) + len(ATT_UNITS) if ffn else 0
                self.fresh = not ffn

            def at(self, n, k):
                return self.s * n + k

            def before(self, n, k):
                return (self.s - 1) * n + k

            def unit(self, name):
                return self.tr0 + self.units.index(name)

        def steps(engine, body):
            body(Step(0, 0, True, False, 0))
            pairs = (BATCH - 2) // 2
            with engine.Fori(0, pairs) as t:
                body(Step(2 * t, 1, True, True, t))
                body(Step(2 * t, 2, True, True, t + 1))
            body(Step(0, BATCH - 1, True, True, BATCH // 2 - 1))
            body(Step(0, BATCH, False, True, BATCH // 2))

        block = ctx.enter_context(nc.Block())

        def batch(view, i):
            return view[bass.ds(i, 1)].rearrange("o p n -> (o p) n") if not isinstance(i, int) else view[i]

        def tview(view, s):
            return view[bass.ds(s, 1)].rearrange("o p k t -> (o p) k t") if not isinstance(s, int) else view[s]

        def heads(t):
            return t.rearrange("p (h d) -> p h d", h=H)

        def spread(t, n):
            return t.rearrange("p (m o) -> p m o", o=1).to_broadcast([P, t.shape[-1], n])

        @block.sync
        def _(sp):
            small = ((bo_sb, bo), (gn, g_norm), (tgx, gate_x), (tgf, gate_f), (tgb, bias), (prio_sb, prio),
                     (bm, BmT), (ar[:, :, 0:ER], AT.rearrange("(k p) n -> p k n", p=P)),
                     (ar[:, :, ER:ER + NE], WrT.rearrange("(k p) n -> p k n", p=P)),
                     (ke[0:DH, 0, :].rearrange("e (h c) -> e h c", h=H), Wv.rearrange("(h e) c -> e h c", e=DH)),
                     (ke[0:DH, 1, :].rearrange("e (h c) -> e h c", h=H), WoT.rearrange("(h e) c -> e h c", e=DH)))
            for dst, src in small:
                sp.dma_start(dst if isinstance(dst, bass.AP) else dst[:, :], src).then_inc(S["const_in"], 16)
            for i in range(W_CHUNKS):
                if i >= 4:
                    sp.wait_ge(S["w_lo"], i - 3)
                src = (WqT, WkT)[i] if i < 2 else WbT[(i - 2) * P:(i - 1) * P, :]
                sp.dma_start(raw[i % 4][:, 0:src.shape[1]], src).then_inc(w_land[i % 4], 16)
                if i < 2:
                    sp.dma_start(c_sb[i][:, :], c_in[i]).then_inc(c_land[i], 16)
                    sp.dma_start(x_sb[i][:, :], x_in[i]).then_inc(x_land[i], 16)

            def body(z):
                if z.att:
                    sp.wait_ge(S["tr_out"], z.unit(("ctx", 1)) + 1)
                    sp.dma_start(tview(ctxT_out, z.s), cT[:, :, :]).then_inc(S["ctxT_st"], 16)
                if z.ffn and z.c != BATCH - 1 and z.c != BATCH:
                    sp.wait_ge(S["x1_done"], z.s)
                    sp.dma_start(x_sb[1 - z.par][:, :], batch(x_in, z.s + 1)).then_inc(x_land[1 - z.par], 16)
                    sp.dma_start(c_sb[1 - z.par][:, :], batch(c_in, z.s + 1)).then_inc(c_land[1 - z.par], 16)
                if z.ffn:
                    sp.wait_ge(S["x2_done"], z.s)
                    sp.dma_start(batch(x_out, z.s - 1), x2[:, :]).then_inc(S["x2_st"], 16)
                    sp.wait_ge(S["tr_out"], z.unit(("n", 1)) + 1)
                    sp.dma_start(tview(xnT_out, z.s - 1), x2T[:, :, :]).then_inc(S["xnT_st"], 16)

            steps(sp, body)
            for n in ("ctxT_st", "x2_st", "xnT_st"):
                sp.wait_ge(S[n], 16 * BATCH)

        @block.gpsimd
        def _(pool):
            def lo(part, src, view=lambda t: t):
                return nc.gpsimd.tensor_tensor(view(part["lo"][:, :]), src, view(part["hi"][:, :]).bitcast(F32),
                                               ALU.subtract)

            nc.gpsimd.memset(eps[:, :], EPS).then_inc(S["const_pool"], 1)
            nc.gpsimd.memset(half_neg[:, :], -0.5).then_inc(S["const_pool"], 1)
            nc.gpsimd.memset(ones[:, :], 1.0).then_inc(S["const_pool"], 1)
            nc.gpsimd.memset(ident[:, :], 0.0).then_inc(S["const_pool"], 1)
            pool.wait_ge(S["const_pool"], 4)
            nc.gpsimd.affine_select(out=ident[:, :], in_=ident[:, :], compare_op=ALU.not_equal, fill=1.0,
                                    base=0, pattern=[[-1, P]], channel_multiplier=1).then_inc(S["const_pool"], 1)
            pool.wait_ge(S["const_in"], 16 * 11)
            pool.wait_ge(S["gates"], 2)
            nc.gpsimd.tensor_scalar(tgb[:, :], tgb[:, :], tgf[:, 0:1], None, ALU.mult).then_inc(S["tgb_done"], 1)
            nc.gpsimd.tensor_scalar(sc[:, :], tgx[:, :], gn[:, 0:1], math.sqrt(SEQ), ALU.mult, ALU.mult)\
                .then_inc(S["sc_done"], 1)
            for i in range(W_CHUNKS):
                pool.wait_ge(S["w_hi"], i + 1)
                if i < 2:
                    lo((wq, wk)[i], raw[i][:, 0:HID]).then_inc(S["w_lo"], 1)
                else:
                    nc.gpsimd.tensor_tensor(wb["lo"][:, i - 2, :], raw[i % 4][:, :],
                                            wb["hi"][:, i - 2, :].bitcast(F32), ALU.subtract).then_inc(S["w_lo"], 1)
            pool.wait_ge(S["tgb_done"], 1)

            def rstd(n, b):
                st, mv, rs = ln[n]
                sems = LN[n]
                pool.wait_ge(sems["mv"], b + 1)
                pool.wait_ge(sems["done"], b)
                nc.gpsimd.tensor_tensor(rs[:, :], mv[:, 1:2], eps[:, :], ALU.add).then_inc(sems["var"], 1)
                pool.wait_ge(sems["var"], b + 1)
                nc.gpsimd.tensor_tensor(rs[:, :], rs[:, :], half_neg[:, 0:1], ALU.pow).then_inc(sems["rstd"], 1)

            def prepare(b, par):
                rstd("x", b)
                pool.wait_ge(S["cc_hi"], b + 1)
                lo(cc, c_sb[par][:, :]).then_inc(S["cc_lo"], 1)
                pool.wait_ge(S["xn_hi"], b + 1)
                lo(xn, xn_f[:, :]).then_inc(S["xn_lo"], 1)

            prepare(0, 0)

            def body(z):
                s = z.s

                def q_norm(r):
                    pool.wait_ge(S["qrec_done"], z.at(KT, r + 1))
                    nc.gpsimd.tensor_tensor(heads(qs[r % 4][:, :]), heads(qs[r % 4][:, :]), spread(qrec[r % 2][:, :], DH),
                                            ALU.mult).then_inc(S["qnorm"], 1)

                if z.ffn:
                    pool.wait_ge(S["ss_out"], s)
                    nc.gpsimd.tensor_tensor(rn[:, :], ss[:, :], half_neg[:, :], ALU.pow).then_inc(S["ss_pow"], 1)
                    pool.wait_ge(S["ss_pow"], s)
                    pool.wait_ge(S["xnT_st"], (s - 1) * 16)
                    nc.gpsimd.tensor_tensor(diag[:, :, :], ident[:, :].rearrange("p (o n) -> p o n", o=1)
                                            .to_broadcast([P, KT, P]), spread(rn[:, :], P), ALU.mult)\
                        .then_inc(S["diag_done"], 1)
                if z.att:
                    q_norm(0)
                if z.ffn:
                    pool.wait_ge(S["t_done"], s)
                    nc.gpsimd.tensor_tensor(x1[:, :], x_sb[1 - z.par][:, :], t_sb[:, :], ALU.add)\
                        .then_inc(S["x1_done"], 1)
                if z.att:
                    q_norm(1)
                if z.ffn:
                    rstd("1", s - 1)
                if z.att:
                    q_norm(2)
                if z.ffn:
                    pool.wait_ge(S["x1_done"], s)
                    nc.gpsimd.tensor_tensor(x1b[:, :], x1[:, :], tgb[:, :], ALU.add).then_inc(S["x1b_done"], 1)
                if z.att:
                    q_norm(3)
                    q_norm(4)
                if z.ffn:
                    pool.wait_ge(S["xT_hi"], s)
                    nc.gpsimd.tensor_tensor(xT["lo"][:, :, :], xT_f[:, :, :], xT["hi"][:, :, :].bitcast(F32),
                                            ALU.subtract).then_inc(S["xT_lo"], 1)
                if z.att:
                    for r in range(5, KT):
                        q_norm(r)
                if z.ffn:
                    rstd("2", s - 1)
                if z.att and z.c != BATCH - 1:
                    prepare(s + 1, 1 - z.par)
                if z.att:
                    pool.wait_ge(S["o_out"], s + 1)
                    pool.wait_ge(LN["1"]["done"], s)
                    nc.gpsimd.tensor_tensor(sq[:, :], o_sb[:, :], o_sb[:, :], ALU.mult).then_inc(S["sq_done"], 1)

            steps(pool, body)

        @block.scalar
        def _(act):
            A = nc.scalar.activation
            act.wait_ge(S["const_in"], 16 * 11)
            A(tgx[:, :], tgx[:, :], ACT.Tanh).then_inc(S["gates"], 1)
            A(tgf[:, :], tgf[:, :], ACT.Tanh).then_inc(S["gates"], 1)
            act.wait_ge(S["avo_done"], 1)
            A(avo[:, :, :], p_k[:, :].rearrange("p (h o) -> p h o", h=H), ACT.Copy).then_inc(S["avo_out"], 1)
            for i in range(W_CHUNKS):
                act.wait_ge(w_land[i % 4], 16 * (i // 4) + 16)
                if i < 2:
                    A((wq, wk)[i]["hi"][:, :], raw[i][:, 0:HID], ACT.Copy).then_inc(S["w_hi"], 1)
                else:
                    A(wb["hi"][:, i - 2, :], raw[i % 4][:, :], ACT.Copy).then_inc(S["w_hi"], 1)
            act.wait_ge(S["sc_done"], 1)

            def prepare(b, par, half):
                act.wait_ge(c_land[par], 16 * half + 16)
                act.wait_ge(S["k_proj"], b * MT)
                A(cc["hi"][:, :], c_sb[par][:, :], ACT.Copy).then_inc(S["cc_hi"], 1)
                act.wait_ge(LN["x"]["done"], b + 1)
                act.wait_ge(S["q_proj"], b * KT)
                A(xn["hi"][:, :], xn_f[:, :], ACT.Copy).then_inc(S["xn_hi"], 1)

            prepare(0, 0, 0)

            def body(z):
                s = z.s

                def copy_out(name):
                    kind, r = name
                    u = z.unit(name)
                    src = p_tr[u % 2 if isinstance(u, int) else z.units.index(name) % 2]
                    t3 = src[:, :].rearrange("p (k n) -> p k n", k=4)
                    dst = {"ctx": lambda: cT[:, 4 * r:4 * r + 4, :],
                           "q": lambda: qT[:, :, r * P:(r + 1) * P],
                           "k": lambda: keT[r % 2][:, :].rearrange("p (k n) -> p k n", k=4),
                           "x": lambda: xT_f[:, 4 * r:4 * r + 4, :],
                           "n": lambda: x2T[:, 4 * r:4 * r + 4, :]}[kind]()
                    act.wait_ge(S["tr_done"], u + 1)
                    A(dst, t3, ACT.Copy).then_inc(S["tr_out"], 1)

                def k_exp(m):
                    act.wait_ge(S["kmax_done"], z.at(MT, m + 1))
                    A(ke[:, m, :], p_k[:, :], ACT.Exp, bias=kneg[:, m:m + 1], accum_out=ksum[:, m:m + 1])\
                        .then_inc(S["kexp"], 1)

                def q_exp(r):
                    act.wait_ge(S["qsub"], z.at(KT, r + 1))
                    A(qs[r % 4][:, :], qs[r % 4][:, :], ACT.Exp).then_inc(S["qexp"], 1)

                if z.att:
                    act.wait_ge(S["ctxT_st"], s * 16)
                    act.wait_ge(S["k_used"], z.at(KT, 0))
                    copy_out(("ctx", 0))
                    copy_out(("ctx", 1))
                    act.wait_ge(S["w2_out"], s)
                for r in range(KT):
                    if z.att:
                        if r % 2 == 0:
                            k_exp(r // 2)
                        q_exp(r)
                        if r == 2:
                            act.wait_ge(S["out_done"], s)
                        if r >= 2:
                            copy_out(("q", r - 2))
                    if z.ffn and r == 4:
                        act.wait_ge(S["lora_done"], s - 1)
                        act.wait_ge(S["xT_lo"], s - 1)
                        act.wait_ge(S["xn_lo"], z.at(1, 1) if z.att else z.s)
                        copy_out(("x", 0))
                        copy_out(("x", 1))
                        act.wait_ge(S["tr_out"], z.unit(("x", 1)) + 1)
                        act.wait_ge(S["y_done"], s - 1)
                        A(xT["hi"][:, :, :], xT_f[:, :, :], ACT.Copy).then_inc(S["xT_hi"], 1)
                    if z.ffn and r == 5:
                        act.wait_ge(S["route_max"], s)
                        A(ex[:, :], p_g[:, ER:ER + NE], ACT.Exp, bias=sm[:, 0:1]).then_inc(S["route_exp"], 1)
                if z.att:
                    copy_out(("q", KT - 2))
                    copy_out(("q", KT - 1))
                    for r in range(6):
                        act.wait_ge(S["k_used"], z.at(KT, max(r - 1, 0)))
                        copy_out(("k", r))
                if z.ffn:
                    act.wait_ge(S["xnT_st"], (s - 1) * 16)
                    copy_out(("n", 0))
                    copy_out(("n", 1))
                if z.att:
                    for r in range(6, KT):
                        act.wait_ge(S["k_used"], z.at(KT, r - 1))
                        copy_out(("k", r))
                    if z.c != BATCH - 1:
                        prepare(s + 1, 1 - z.par, z.half + (1 if z.par else 0))
                    act.wait_ge(S["k_used"], z.at(KT, KT))
                    A(g_sb[:, :], p_g[:, :], ACT.Copy).then_inc(S["g_out"], 1)
                    act.wait_ge(S["out_done"], s + 1)
                    act.wait_ge(S["t_done"], s)
                    act.wait_ge(S["sq_done"], s)
                    A(o_sb[:, :], p_k[:, :], ACT.Identity, bias=bo_sb[:, 0:1]).then_inc(S["o_out"], 1)

            steps(act, body)

        @block.vector
        def _(dve):
            V = nc.vector

            def norm(n, src, dst, b, free):
                st, mv, rs = ln[n]
                sems = LN[n]
                dve.wait_ge(sems["mv"], b)
                for h in range(2):
                    V.bn_stats(st[:, h, :], src[:, h * BANK:(h + 1) * BANK]).then_inc(sems["stats"], 1)
                dve.wait_ge(sems["stats"], 2 * b + 2)
                dve.wait_ge(sems["done"], b)
                dve.sem_inc(S["norm_steps"], 1)
                V.bn_aggr(mv[:, :], st[:, :, :]).then_inc(sems["mv"], 1)

            def norm_apply(n, src, dst, b):
                st, mv, rs = ln[n]
                dve.wait_ge(LN[n]["rstd"], b + 1)
                V.tensor_scalar(dst[:, :], src[:, :], mv[:, 0:1], rs[:, 0:1], ALU.subtract, ALU.mult)\
                    .then_inc(LN[n]["done"], 1)

            def prepare(b, par, half):
                dve.wait_ge(x_land[par], 16 * half + 16)
                norm("x", x_sb[par], xn_f, b, None)

            def prepare_apply(b, par, ffn=0):
                dve.wait_ge(S["xn_lo"], b)
                if not isinstance(ffn, int) or ffn > 0:
                    dve.wait_ge(S["xT_lo"], ffn)
                    dve.wait_ge(S["lora_done"], ffn)
                norm_apply("x", x_sb[par], xn_f, b)

            prepare(0, 0, 0)
            prepare_apply(0, 0)

            def body(z):
                s = z.s

                def k_max(m):
                    dve.wait_ge(S["k_proj"], z.at(MT, m + 1))
                    dve.wait_ge(S["kexp"], z.at(MT, m))
                    V.tensor_reduce(kneg[:, m:m + 1], p_k[:, :], AX.X, ALU.max, negate=True)\
                        .then_inc(S["kmax_done"], 1)

                def q_shift(r):
                    dve.wait_ge(S["q_proj"], z.at(KT, r + 1))
                    dve.wait_ge(S["qsub"], z.at(KT, r))
                    V.tensor_reduce(qmax[:, :], heads(p_q[:, :]), AX.X, ALU.max).then_inc(S["qmax_done"], 1)
                    dve.wait_ge(S["qmax_done"], z.at(KT, r + 1))
                    if r >= 4:
                        dve.wait_ge(S["tr_done"], z.unit(("q", r - 4)) + 1)
                    V.tensor_tensor(heads(qs[r % 4][:, :]), heads(p_q[:, :]), spread(qmax[:, :], DH), ALU.subtract)\
                        .then_inc(S["qsub"], 1)

                def q_total(r):
                    dve.wait_ge(S["qexp"], z.at(KT, r + 1))
                    dve.wait_ge(S["qrec_done"], z.at(KT, r))
                    V.tensor_reduce(qsum[:, :], heads(qs[r % 4][:, :]), AX.X, ALU.add).then_inc(S["qsum_done"], 1)
                    dve.wait_ge(S["qsum_done"], z.at(KT, r + 1))
                    dve.wait_ge(S["qnorm"], z.at(KT, max(r - 1, 0)))
                    V.reciprocal(qrec[r % 2][:, :], qsum[:, :]).then_inc(S["qrec_done"], 1)

                def tiny(k):
                    dve.wait_ge(S["route_step"], z.before(12, k))

                if z.ffn:
                    dve.wait_ge(S["ss_done"], s)
                    dve.wait_ge(S["ss_pow"], s - 1)
                    V.tensor_scalar(ss[:, :], p_g[:, 0:KT], 1e-24, None, ALU.max).then_inc(S["ss_out"], 1)
                for r in range(KT):
                    if z.att:
                        if r % 2 == 0:
                            k_max(r // 2)
                        q_shift(r)
                        if r >= 1:
                            q_total(r - 1)
                    if z.ffn and r == 0:
                        dve.wait_ge(S["spread_done"], s)
                        dve.wait_ge(S["x1_done"], s - 1)
                        V.scalar_tensor_tensor(out=t_sb[:, :], in0=o_sb[:, :], scalar=sc[:, 0:1], in1=p_y[:, :],
                                               op0=ALU.mult, op1=ALU.mult).then_inc(S["t_done"], 1)
                    if z.ffn and r == 1:
                        dve.wait_ge(S["x1_done"], s)
                        norm("1", x1, t_sb, s - 1, None)
                    if z.ffn and r == 2:
                        norm_apply("1", x1, t_sb, s - 1)
                    if z.ffn and r == 5:
                        dve.wait_ge(S["lora_done"], s)
                        tiny(0)
                        V.tensor_reduce(sm[:, 0:1], p_g[:, ER:ER + NE], AX.X, ALU.max, negate=True)\
                            .then_inc(S["route_max"], 1)
                        dve.wait_ge(S["route_exp"], s)
                        V.tensor_reduce(sm[:, 1:2], ex[:, :], AX.X, ALU.max).then_inc(S["route_step"], 1)
                        tiny(1)
                        V.scalar_tensor_tensor(out=tmp[:, :], in0=ex[:, :], scalar=sm[:, 1:2], in1=prio_sb[:, :],
                                               op0=ALU.is_equal, op1=ALU.mult).then_inc(S["route_step"], 1)
                        tiny(2)
                        V.tensor_reduce(sm[:, 2:3], tmp[:, :], AX.X, ALU.max).then_inc(S["route_step"], 1)
                        tiny(3)
                        V.tensor_scalar(sel[:, :], prio_sb[:, :], sm[:, 2:3], None, ALU.is_equal)\
                            .then_inc(S["route_step"], 1)
                        tiny(4)
                        V.scalar_tensor_tensor(out=rt[:, :], in0=sel[:, :], scalar=-4.0, in1=ex[:, :],
                                               op0=ALU.mult, op1=ALU.add).then_inc(S["route_step"], 1)
                        tiny(5)
                        V.tensor_reduce(sm[:, 3:4], rt[:, :], AX.X, ALU.max).then_inc(S["route_step"], 1)
                        tiny(6)
                        V.scalar_tensor_tensor(out=tmp[:, :], in0=rt[:, :], scalar=sm[:, 3:4], in1=prio_sb[:, :],
                                               op0=ALU.is_equal, op1=ALU.mult).then_inc(S["route_step"], 1)
                        tiny(7)
                        V.tensor_reduce(sm[:, 4:5], tmp[:, :], AX.X, ALU.max).then_inc(S["route_step"], 1)
                        tiny(8)
                        V.scalar_tensor_tensor(out=sel[:, :], in0=prio_sb[:, :], scalar=sm[:, 4:5], in1=sel[:, :],
                                               op0=ALU.is_equal, op1=ALU.add).then_inc(S["route_step"], 1)
                        V.tensor_tensor(sm[:, 5:6], sm[:, 1:2], sm[:, 3:4], ALU.add).then_inc(S["route_step"], 1)
                        tiny(10)
                        V.reciprocal(sm[:, 6:7], sm[:, 5:6]).then_inc(S["route_step"], 1)
                        V.tensor_tensor(rt[:, :], ex[:, :], sel[:, :], ALU.mult).then_inc(S["route_step"], 1)
                        tiny(12)
                        V.tensor_scalar(rt[:, :], rt[:, :], sm[:, 6:7], 2.0, ALU.mult, ALU.mult)\
                            .then_inc(S["rt_done"], 1)
                        dve.wait_ge(S["rt_done"], s)
                        dve.wait_ge(S["h_turned"], s - 1)
                        V.tensor_tensor(h_sb[:, :].rearrange("p (e r) -> p e r", e=NE),
                                        p_g[:, 0:ER].rearrange("p (e r) -> p e r", e=NE), spread(rt[:, :], R),
                                        ALU.mult).then_inc(S["h_done"], 1)
                    if z.ffn and r == 6:
                        dve.wait_ge(S["h_turned"], s)
                        dve.wait_ge(S["y_done"], s - 1)
                        V.tensor_copy(hT[:, :], p_g[:, 2 * P:3 * P]).then_inc(S["hT_out"], 1)
                if z.att:
                    q_total(KT - 1)
                    dve.wait_ge(S["w2_out"], s)
                    dve.wait_ge(S["kexp"], z.at(MT, MT))
                    V.reciprocal(krec[:, :], ksum[:, :]).then_inc(S["krec_done"], 1)
                if z.ffn:
                    dve.wait_ge(S["y_done"], s)
                    dve.wait_ge(S["x1b_done"], s)
                    dve.wait_ge(S["x2_st"], (s - 1) * 16)
                    V.scalar_tensor_tensor(out=x2[:, :], in0=p_y[:, :], scalar=tgf[:, 0:1], in1=x1b[:, :],
                                           op0=ALU.mult, op1=ALU.add).then_inc(S["x2_done"], 1)
                    dve.wait_ge(S["x2_done"], s)
                    norm("2", x2, t_sb, s - 1, None)
                    norm_apply("2", x2, t_sb, s - 1)
                if z.att:
                    if z.c != BATCH - 1:
                        prepare(s + 1, 1 - z.par, z.half + (1 if z.par else 0))
                        prepare_apply(s + 1, 1 - z.par, s)
                    dve.wait_ge(S["krec_done"], s + 1)
                    dve.wait_ge(S["w2_done"], s + 1)
                    V.scalar_tensor_tensor(out=w2[:, :, :], in0=p_g[:, :].rearrange("p (m o) -> p m o", m=MT),
                                           scalar=DH ** -0.5, in1=spread(krec[:, :], P), op0=ALU.mult, op1=ALU.mult)\
                        .then_inc(S["w2_out"], 1)

            steps(dve, body)

        @block.tensor
        def _(pe):
            M, T = nc.tensor.matmul, nc.tensor.transpose

            pe.wait_ge(S["const_pool"], 5)
            pe.wait_ge(S["const_in"], 16 * 11)
            for h in range(H):
                mm = M(p_k[:, h * P:(h + 1) * P], ke[0:DH, 0, h * P:(h + 1) * P], ke[0:DH, 1, h * P:(h + 1) * P],
                       start=True, stop=True)
            mm.then_inc(S["avo_done"], 1)
            pe.wait_ge(S["avo_out"], 1)

            def body(z):
                s = z.s

                def turn(name):
                    kind, r = name
                    i = z.units.index(name)
                    u = z.unit(name)
                    if not (z.fresh and i < 2):
                        pe.wait_ge(S["tr_out"], u - 1)
                    for m in range(4):
                        k = 4 * r + m
                        src = {"ctx": lambda: c_sb[z.par][:, k * P:(k + 1) * P],
                               "q": lambda: qs[r % 4][:, m * P:(m + 1) * P],
                               "k": lambda: ke[:, m, r * P:(r + 1) * P],
                               "x": lambda: t_sb[:, k * P:(k + 1) * P],
                               "n": lambda: t_sb[:, k * P:(k + 1) * P]}[kind]()
                        mm = T(p_tr[i % 2][:, m * P:(m + 1) * P], src, ident[:, :])
                    mm.then_inc(S["tr_done"], 1)

                def k_project(m):
                    if m == 0:
                        pe.wait_ge(S["cc_lo"], s + 1)
                        pe.wait_ge(S["o_out"], s)
                    else:
                        pe.wait_ge(S["kexp"], z.at(MT, m))
                    for h in range(2):
                        for n, (a, b) in enumerate(SPLIT):
                            mm = M(p_k[:, h * BANK:(h + 1) * BANK], wk[a][:, m * P:(m + 1) * P],
                                   cc[b][:, h * BANK:(h + 1) * BANK], start=(n == 0), stop=(n == 2))
                    mm.then_inc(S["k_proj"], 1)

                def q_project(r):
                    if r == 0:
                        pe.wait_ge(S["xn_lo"], s + 1)
                    pe.wait_ge(S["qsub"], z.at(KT, r))
                    for n, (a, b) in enumerate(SPLIT):
                        mm = M(p_q[:, :], xn[a][:, r * P:(r + 1) * P], wq[b][:, :], start=(n == 0), stop=(n == 2))
                    mm.then_inc(S["q_proj"], 1)

                def base(ks):
                    for k in ks:
                        for h in range(2):
                            for n, (a, b) in enumerate(SPLIT):
                                M(p_y[:, h * BANK:(h + 1) * BANK], xT[a][:, k, :], wb[b][:, k, h * BANK:(h + 1) * BANK],
                                  start=(k == 0 and n == 0), stop=False)

                def gather(r):
                    pe.wait_ge(S["tr_out"], z.unit(("k", r)) + 1)
                    M(p_g[:, :], cT[:, r, :], keT[r % 2][:, :], start=(r == 0), stop=(r == KT - 1))\
                        .then_inc(S["k_used"], 1)

                if z.ffn:
                    pe.wait_ge(S["sq_done"], s)
                    pe.wait_ge(S["w2_out"], s)
                    for r in range(KT):
                        mm = M(p_g[:, r:r + 1], sq[:, r * P:(r + 1) * P], ones[:, 0:1], start=True, stop=True)
                    mm.then_inc(S["ss_done"], 1)
                if z.att:
                    pe.wait_ge(c_land[z.par], 16 * z.half + 16)
                    turn(("ctx", 0))
                    turn(("ctx", 1))
                for r in range(KT):
                    if z.att:
                        if r % 2 == 0:
                            k_project(r // 2)
                        q_project(r)
                    if z.ffn and r == 0:
                        pe.wait_ge(S["diag_done"], s)
                        pe.wait_ge(S["x2_done"], s - 1)
                        for h in range(2):
                            mm = M(p_y[:, h * BANK:(h + 1) * BANK], ones[:, :], diag[:, 4 * h:4 * h + 4, :],
                                   start=True, stop=True)
                        mm.then_inc(S["spread_done"], 1)
                    if z.att and r >= 2:
                        pe.wait_ge(S["qnorm"], z.at(KT, r - 1))
                        turn(("q", r - 2))
                    if z.ffn and r == 4:
                        pe.wait_ge(LN["1"]["done"], s)
                        turn(("x", 0))
                        turn(("x", 1))
                    if z.ffn and r == 5:
                        pe.wait_ge(S["tr_out"], z.unit(("x", 1)) + 1)
                        pe.wait_ge(S["ss_out"], s)
                        for k in range(KT):
                            mm = M(p_g[:, 0:ER + NE], xT_f[:, k, :], ar[:, k, :], start=(k == 0), stop=(k == KT - 1))
                        mm.then_inc(S["lora_done"], 1)
                        pe.wait_ge(S["t_done"], s)
                        pe.wait_ge(S["xT_lo"], s)
                        base(range(0, 2))
                    if z.ffn and r == 6:
                        base(range(2, 4))
                        pe.wait_ge(S["h_done"], s)
                        T(p_g[:, 2 * P:3 * P], h_sb[:, :], ident[:, :]).then_inc(S["h_turned"], 1)
                    if z.ffn and r == 7:
                        base(range(4, 6))
                if z.att:
                    pe.wait_ge(S["qnorm"], z.at(KT, KT - 1))
                    turn(("q", KT - 2))
                if z.ffn:
                    base(range(6, 8))
                    pe.wait_ge(S["hT_out"], s)
                    for h in range(2):
                        mm = M(p_y[:, h * BANK:(h + 1) * BANK], hT[:, :], bm[:, h * BANK:(h + 1) * BANK],
                               start=False, stop=True)
                    mm.then_inc(S["y_done"], 1)
                if z.att:
                    pe.wait_ge(S["qnorm"], z.at(KT, KT))
                    turn(("q", KT - 1))
                    pe.wait_ge(S["kexp"], z.at(MT, MT))
                    turn(("k", 0))
                    for r in range(1, 6):
                        turn(("k", r))
                        gather(r - 1)
                if z.ffn:
                    pe.wait_ge(LN["2"]["done"], s)
                    turn(("n", 0))
                    turn(("n", 1))
                if z.att:
                    for r in range(6, KT):
                        turn(("k", r))
                        gather(r - 1)
                    gather(KT - 1)
                    pe.wait_ge(S["g_out"], s + 1)
                    for h in range(H):
                        half = slice(DH * (h % 2), DH * (h % 2) + DH)
                        mm = M(p_g[half, (h // 2) * P:(h // 2 + 1) * P], g_sb[:, h * DH:(h + 1) * DH], avo[:, h, :],
                               start=True, stop=True)
                    mm.then_inc(S["w2_done"], 1)
                    pe.wait_ge(S["w2_out"], s + 1)
                    pe.wait_ge(S["tr_out"], z.unit(("q", KT - 1)) + 1)
                    for h in range(2):
                        for m in range(MT):
                            mm = M(p_k[:, h * BANK:(h + 1) * BANK], w2[:, m, :], qT[:, m, h * BANK:(h + 1) * BANK],
                                   start=(m == 0), stop=(m == MT - 1))
                    mm.then_inc(S["out_done"], 1)

            steps(pe, body)


def gqa_stage(nc, x_in, xnT, ctxT, mask, gate, Wq, Wk, Wv, Wo, cos_t, sin_t, x_out):
    HD, NH, NKV = 128, 32, 8
    G = NH // NKV
    NB = BANK // SEQ
    NGRP = BATCH // NB
    CAP = 30.0
    SCALE = 0.08838834764831845 / CAP
    CH = 1024
    C_ACT, C_WO, C_WKV, C_WQ = 8, 4, 2, 4
    C_PRE = C_WKV + C_WQ
    C_IT = C_WO + C_PRE
    C_GRP = C_ACT + NKV * C_IT
    NR = 1 + G
    NU = NB * (DM // BANK)

    with ExitStack() as ctx:
        def sb(name, shape, dt=F32):
            return ctx.enter_context(nc.sbuf_tensor("g_" + name, shape, dt))

        def ps(name):
            return ctx.enter_context(nc.psum_tensor("gp_" + name, [P, BANK], F32))

        def sem(name):
            return ctx.enter_context(nc.semaphore("g_" + name))

        def pair(name, shape):
            return {h: sb(f"{name}_{h}", shape, F32R) for h in ("hi", "lo")}

        xn = pair("xn", [P, KT, BANK])
        cx = pair("cx", [P, KT, BANK])
        wq = pair("wq", [P, KT, G * HD])
        wk = pair("wk", [P, KT, HD])
        wv = pair("wv", [P, KT, HD])
        wo = pair("wo", [P, G, DM])
        at = pair("at", [P, G, BANK])
        raw = [sb(f"raw{i}", [P, CH]) for i in range(2)]
        res = sb("res", [P, NB, DM])
        q_sb = sb("q_sb", [P, G, BANK])
        k_sb = sb("k_sb", [P, BANK])
        v_sb = sb("v_sb", [P, BANK])
        rot_b = [sb(f"rot_b{i}", [P, BANK]) for i in range(2)]
        prob = [sb(f"prob{i}", [P, BANK]) for i in range(2)]
        vT = prob[0]
        rsum = rot_b[1]
        attn = q_sb
        cos_sb = sb("cos", [P, SEQ])
        sin_sb = sb("sin", [P, SEQ])
        m8 = sb("m8", [P, SEQ // 4], U32)
        mf = k_sb[:, 0:SEQ]
        keep = sb("keep", [P, SEQ])
        empty = sb("empty", [P, SEQ])
        ident = sb("ident", [P, P])
        ones = sb("ones", [P, P])
        tg = sb("tg", [P, 1])

        p_proj = [ps("p0"), ps("p1")]
        p_s, p_pv, p_sum = ps("ps"), ps("pv"), ps("sum")
        p_y = [ps("y0"), ps("y1"), ps("y2")]
        unit_bank = [p_y[0], p_y[1], p_y[2], p_proj[0], p_proj[1], p_y[0], p_y[1], p_y[2]]

        const_in = sem("const_in")
        const_pool = sem("const_pool")
        const_dve = sem("const_dve")
        const_pe = sem("const_pe")
        gate_done = sem("gate_done")
        landed = [sem(f"landed{i}") for i in range(2)]
        split_hi = sem("split_hi")
        split_lo = sem("split_lo")
        res_in = sem("res_in")
        res_out = sem("res_out")
        qk_proj = sem("qk_proj")
        v_proj = sem("v_proj")
        vT_out = sem("vT_out")
        v_turned = sem("v_turned")
        v_ready = sem("v_ready")
        rot_mul = sem("rot_mul")
        rot_done = sem("rot_done")
        s_done = sem("s_done")
        tanh_done = sem("tanh_done")
        exp_done = sem("exp_done")
        masked = sem("masked")
        prob_ready = sem("prob_ready")
        sum_done = sem("sum_done")
        pv_done = sem("pv_done")
        rsum_done = sem("rsum_done")
        attn_done = sem("attn_done")
        at_hi = sem("at_hi")
        at_lo = sem("at_lo")
        y_done = sem("y_done")
        y_added = sem("y_added")

        Wq_v = Wq.rearrange("(k p) (j n) -> j p k n", p=P, j=NKV)
        Wk_v = Wk.rearrange("(k p) (j n) -> j p k n", p=P, j=NKV)
        Wv_v = Wv.rearrange("(k p) (j n) -> j p k n", p=P, j=NKV)
        Wo_v = Wo.rearrange("(j g p) n -> j p g n", p=P, j=NKV)
        res_src = x_in.rearrange("(g b) t d -> g t b d", b=NB)
        res_dst = x_out.rearrange("(g b) t d -> g t b d", b=NB)

        block = ctx.enter_context(nc.Block())

        def one(view, i):
            return view[bass.ds(i, 1)].rearrange("o p k n -> (o p) k n")

        def acts():
            for i in range(C_ACT):
                yield i, (xn, cx)[i // NB], (lambda t, i=i: t[:, :, (i % NB) * SEQ:(i % NB + 1) * SEQ])

        def outs():
            for i in range(C_WO):
                yield i, wo, (lambda t, i=i: t[:, i:i + 1, :])

        def ahead(c0):
            yield c0, wk, (lambda t: t[:, :, :])
            yield c0 + 1, wv, (lambda t: t[:, :, :])
            for i in range(C_WQ):
                yield c0 + 2 + i, wq, (lambda t, i=i: t[:, 2 * i:2 * i + 2, :])

        def raw_view(c, like):
            return raw[c % 2][:, :].rearrange("p (k n) -> p k n", n=like.shape[-1])

        def wide(t):
            return t[:, :].rearrange("p (o t) -> p o t", o=1).to_broadcast([P, NB, SEQ])

        @block.sync
        def _(sp):
            def stage(c, base, src, first=False):
                if not first:
                    sp.wait_ge(split_lo, base + c - 1)
                dst = raw[c % 2][:, :].rearrange("p (k n) -> p k n", n=src.shape[-1])
                sp.dma_start(dst, src).then_inc(landed[c % 2], 16)

            def weights_ahead(base, j, c0, first=False):
                stage(c0, base, one(Wk_v, j), first)
                stage(c0 + 1, base, one(Wv_v, j), first)
                for i in range(C_WQ):
                    stage(c0 + 2 + i, base, one(Wq_v, j)[:, 2 * i:2 * i + 2, :])

            sp.dma_start(cos_sb[:, :], cos_t).then_inc(const_in, 16)
            sp.dma_start(sin_sb[:, :], sin_t).then_inc(const_in, 16)
            sp.dma_start(m8[:, :], mask).then_inc(const_in, 16)
            sp.dma_start(tg[:, :], gate).then_inc(const_in, 16)
            weights_ahead(0, 0, 0, first=True)
            with sp.Fori(0, NGRP) as g:
                for i in range(C_ACT):
                    stage(i, g * C_GRP + C_PRE, one((xnT, ctxT)[i // NB], g * NB + i % NB))
                sp.wait_ge(res_out, 16 * g)
                sp.dma_start(res[:, :, :], one(res_src, g)).then_inc(res_in, 16)
                with sp.Fori(0, NKV) as j:
                    base = g * C_GRP + j * C_IT + C_PRE + C_ACT
                    for i in range(C_WO):
                        stage(i, base, one(Wo_v, j)[:, i:i + 1, :])
                    weights_ahead(base, (j + 1) % NKV, C_WO)
                sp.wait_ge(y_added, (g + 1) * NKV * NU)
                sp.dma_start(one(res_dst, g), res[:, :, :]).then_inc(res_out, 16)
            sp.wait_ge(res_out, 16 * NGRP)

        @block.gpsimd
        def _(pool):
            def lo(c, base, part, view):
                pool.wait_ge(split_hi, base + c + 1)
                nc.gpsimd.tensor_tensor(view(part["lo"]), raw_view(c, view(part["lo"])),
                                        view(part["hi"]).bitcast(F32), ALU.subtract).then_inc(split_lo, 1)

            nc.gpsimd.memset(ones[:, :], 1.0).then_inc(const_pool, 1)
            nc.gpsimd.memset(ident[:, :], 0.0).then_inc(const_pool, 1)
            pool.wait_ge(const_pool, 2)
            nc.gpsimd.affine_select(out=ident[:, :], in_=ident[:, :], compare_op=ALU.not_equal, fill=1.0,
                                    base=0, pattern=[[-1, P]], channel_multiplier=1).then_inc(const_pool, 1)
            for c, part, view in ahead(0):
                lo(c, 0, part, view)
            with pool.Fori(0, NGRP) as g:
                for c, part, view in acts():
                    lo(c, g * C_GRP + C_PRE, part, view)
                with pool.Fori(0, NKV) as j:
                    n = g * NKV + j
                    base = g * C_GRP + j * C_IT + C_PRE + C_ACT

                    def rotate(i):
                        pool.wait_ge(rot_mul, n * NR + i + 1)
                        dst = k_sb[:, :] if i == 0 else q_sb[:, i - 1, :]
                        nc.gpsimd.tensor_tensor(dst, dst, rot_b[i % 2][:, :], ALU.add)\
                            .then_inc(rot_done, 1)

                    def mask_probs(h):
                        e = prob[h % 2][:, :].rearrange("p (b t) -> p b t", b=NB)
                        pool.wait_ge(exp_done, n * G + h + 1)
                        nc.gpsimd.tensor_tensor(e, e, wide(keep), ALU.mult).then_inc(masked, 1)
                        pool.wait_ge(masked, n * G + h + 1)
                        nc.gpsimd.tensor_tensor(e, e, wide(empty), ALU.add).then_inc(prob_ready, 1)

                    def attn_lo(h):
                        pool.wait_ge(at_hi, n * G + h + 1)
                        nc.gpsimd.tensor_tensor(at["lo"][:, h, :], attn[:, h, :], at["hi"][:, h, :].bitcast(F32),
                                                ALU.subtract).then_inc(at_lo, 1)

                    out_w = list(outs())
                    nxt = list(ahead(C_WO))
                    for c, part, view in out_w:
                        lo(c, base, part, view)
                    rotate(0)
                    for c, part, view in nxt[:C_WKV]:
                        lo(c, base, part, view)
                    rotate(1)
                    rotate(2)
                    pool.wait_ge(const_dve, 3)
                    mask_probs(0)
                    rotate(3)
                    mask_probs(1)
                    attn_lo(0)
                    rotate(4)
                    mask_probs(2)
                    attn_lo(1)
                    mask_probs(3)
                    attn_lo(2)
                    for c, part, view in nxt[C_WKV:C_WKV + 2]:
                        lo(c, base, part, view)
                    attn_lo(3)
                    for c, part, view in nxt[C_WKV + 2:]:
                        lo(c, base, part, view)

        @block.scalar
        def _(act):
            def hi(c, base, half, part, view):
                act.wait_ge(landed[c % 2], half * 16 + 16 * (c // 2 + 1))
                nc.scalar.activation(view(part["hi"]), raw_view(c, view(part["hi"])), ACT.Copy)\
                    .then_inc(split_hi, 1)

            act.wait_ge(const_in, 64)
            nc.scalar.activation(tg[:, :], tg[:, :], ACT.Tanh).then_inc(gate_done, 1)
            for c, part, view in ahead(0):
                hi(c, 0, 0, part, view)
            with act.Fori(0, NGRP) as g:
                act.wait_ge(qk_proj, g * NKV * NR)
                for c, part, view in acts():
                    hi(c, None, g * (C_GRP // 2) + C_PRE // 2, part, view)
                with act.Fori(0, NKV) as j:
                    n = g * NKV + j
                    half = g * (C_GRP // 2) + j * (C_IT // 2) + (C_PRE + C_ACT) // 2

                    def probs(h):
                        e = prob[h % 2][:, :]
                        act.wait_ge(s_done, n * G + h + 1)
                        act.wait_ge(pv_done, n * G + max(h - 1, 0))
                        nc.scalar.activation(e, p_s[:, :], ACT.Tanh, scale=SCALE).then_inc(tanh_done, 1)
                        act.wait_ge(tanh_done, n * G + h + 1)
                        nc.scalar.activation(e, e, ACT.Exp, scale=CAP).then_inc(exp_done, 1)

                    def attn_hi(h):
                        act.wait_ge(attn_done, n * G + h + 1)
                        nc.scalar.activation(at["hi"][:, h, :], attn[:, h, :], ACT.Copy).then_inc(at_hi, 1)

                    nxt = list(ahead(C_WO))
                    act.wait_ge(y_done, n * NU)
                    for c, part, view in outs():
                        hi(c, None, half, part, view)
                    act.wait_ge(v_proj, n + 1)
                    nc.scalar.activation(vT[:, :], p_proj[1][:, :], ACT.Copy).then_inc(vT_out, 1)
                    for c, part, view in nxt[:C_WKV]:
                        hi(c, None, half, part, view)
                    act.wait_ge(v_turned, n + 1)
                    nc.scalar.activation(v_sb[:, :], p_s[:, :], ACT.Copy).then_inc(v_ready, 1)
                    probs(0)
                    probs(1)
                    attn_hi(0)
                    probs(2)
                    attn_hi(1)
                    probs(3)
                    attn_hi(2)
                    act.wait_ge(qk_proj, n * NR + NR)
                    for c, part, view in nxt[C_WKV:C_WKV + 2]:
                        hi(c, None, half, part, view)
                    attn_hi(3)
                    for c, part, view in nxt[C_WKV + 2:]:
                        hi(c, None, half, part, view)

        @block.vector
        def _(dve):
            dve.wait_ge(const_in, 64)
            nc.vector.tensor_copy(mf, m8[:, :].bitcast(U8)).then_inc(const_dve, 1)
            dve.wait_ge(const_pe, 1)
            nc.vector.tensor_copy(keep[:, :], p_s[:, 0:SEQ]).then_inc(const_dve, 1)
            dve.wait_ge(const_pe, 2)
            nc.vector.tensor_scalar(empty[:, :], p_s[:, 0:SEQ], 0.5, None, ALU.is_lt).then_inc(const_dve, 1)
            dve.wait_ge(gate_done, 1)
            with dve.Fori(0, NGRP) as g:
                with dve.Fori(0, NKV) as j:
                    n = g * NKV + j

                    def rotate(i):
                        src = p_proj[0 if i == 0 else (i - 1) % 2]
                        a, b = (k_sb if i == 0 else q_sb[:, i - 1, :]), rot_b[i % 2]
                        half = P // 2
                        dve.wait_ge(qk_proj, n * NR + i + 1)
                        dve.wait_ge(rot_done, n * NR + max(i - 1, 0))
                        if i == 0:
                            dve.wait_ge(s_done, n * G)
                            dve.wait_ge(at_lo, n * G)

                        def v(t, lo_, hi_):
                            return t[lo_:hi_, :].rearrange("p (b t) -> p b t", b=NB)

                        def w(t, lo_, hi_):
                            return t[lo_:hi_, :].rearrange("p (o t) -> p o t", o=1).to_broadcast([hi_ - lo_, NB, SEQ])

                        nc.vector.tensor_tensor(v(a, 0, P), v(src, 0, P), w(cos_sb, 0, P), ALU.mult)
                        nc.vector.tensor_tensor(v(b, half, P), v(src, 0, half), w(sin_sb, 0, half), ALU.mult)
                        nc.vector.tensor_tensor(v(b, 0, half), v(src, half, P), w(sin_sb, half, P), ALU.mult)\
                            .then_inc(rot_mul, 1)

                    def normalise(h):
                        dve.wait_ge(sum_done, n * G + h + 1)
                        dve.wait_ge(rot_done, n * NR + NR - 1)
                        nc.vector.reciprocal(rsum[:, :], p_sum[:, :]).then_inc(rsum_done, 1)
                        dve.wait_ge(rsum_done, n * G + h + 1)
                        dve.wait_ge(pv_done, n * G + h + 1)
                        nc.vector.tensor_tensor(attn[:, h, :], p_pv[:, :], rsum[:, :], ALU.mult).then_inc(attn_done, 1)

                    rotate(0)
                    rotate(1)
                    rotate(2)
                    rotate(3)
                    normalise(0)
                    rotate(4)
                    for h in range(1, G):
                        normalise(h)
                    dve.wait_ge(res_in, 16 * g + 16)
                    dve.wait_ge(y_added, n * NU)
                    for u in range(NU):
                        b, h = u // 2, u % 2
                        r = res[:, b, h * BANK:(h + 1) * BANK]
                        dve.wait_ge(y_done, n * NU + u + 1)
                        nc.vector.scalar_tensor_tensor(out=r, in0=unit_bank[u][:, :], scalar=tg[:, 0:1], in1=r,
                                                       op0=ALU.mult, op1=ALU.add).then_inc(y_added, 1)

        @block.tensor
        def _(pe):
            def projection(bank, w, cols, x):
                for k in range(KT):
                    for t, (a, b) in enumerate(SPLIT):
                        mm = nc.tensor.matmul(bank[:, :], w[a][:, k, cols], x[b][:, k, :],
                                              start=(k == 0 and t == 0), stop=(k == KT - 1 and t == 2))
                return mm

            pe.wait_ge(const_dve, 1)
            pe.wait_ge(const_pool, 3)
            nc.tensor.transpose(p_s[:, 0:P], mf, ident[:, :]).then_inc(const_pe, 1)
            pe.wait_ge(const_dve, 2)
            nc.tensor.matmul(p_s[:, 0:SEQ], ones[:, :], keep[:, :], start=True, stop=True).then_inc(const_pe, 1)
            pe.wait_ge(const_dve, 3)
            with pe.Fori(0, NGRP) as g:
                with pe.Fori(0, NKV) as j:
                    n = g * NKV + j
                    base = g * C_GRP + j * C_IT + C_PRE + C_ACT

                    def query(h):
                        if h == 1:
                            pe.wait_ge(vT_out, n + 1)
                        else:
                            pe.wait_ge(rot_mul, n * NR + max(h, 1))
                        projection(p_proj[h % 2], wq, slice(h * HD, (h + 1) * HD), xn).then_inc(qk_proj, 1)

                    def scores(h):
                        pe.wait_ge(rot_done, n * NR + h + 2)
                        if h == 0:
                            pe.wait_ge(v_ready, n + 1)
                        pe.wait_ge(tanh_done, n * G + h)
                        for b in range(NB):
                            cols = slice(b * SEQ, (b + 1) * SEQ)
                            mm = nc.tensor.matmul(p_s[:, cols], k_sb[:, cols], q_sb[:, h, cols],
                                                  start=True, stop=True)
                        mm.then_inc(s_done, 1)

                    def values(h):
                        pe.wait_ge(prob_ready, n * G + h + 1)
                        pe.wait_ge(attn_done, n * G + h)
                        nc.tensor.matmul(p_sum[:, :], ones[:, :], prob[h % 2][:, :], start=True, stop=True)\
                            .then_inc(sum_done, 1)
                        for b in range(NB):
                            cols = slice(b * SEQ, (b + 1) * SEQ)
                            mm = nc.tensor.matmul(p_pv[:, cols], v_sb[:, cols], prob[h % 2][:, cols],
                                                  start=True, stop=True)
                        mm.then_inc(pv_done, 1)

                    def out_part(units, h):
                        pe.wait_ge(at_lo, n * G + h + 1)
                        for u in units:
                            b, half = u // 2, u % 2
                            if h == 0:
                                pe.wait_ge(y_added, n * NU + max(u - 4, 0))
                            for t, (p, r) in enumerate(SPLIT):
                                mm = nc.tensor.matmul(unit_bank[u][:, :], at[p][:, h, b * SEQ:(b + 1) * SEQ],
                                                      wo[r][:, h, half * BANK:(half + 1) * BANK],
                                                      start=(h == 0 and t == 0), stop=(h == G - 1 and t == 2))
                            if h == G - 1:
                                mm.then_inc(y_done, 1)

                    pe.wait_ge(split_lo, base)
                    pe.wait_ge(y_added, n * NU)
                    projection(p_proj[0], wk, slice(0, HD), cx).then_inc(qk_proj, 1)
                    projection(p_proj[1], wv, slice(0, HD), cx).then_inc(v_proj, 1)
                    query(0)
                    pe.wait_ge(vT_out, n + 1)
                    pe.wait_ge(tanh_done, n * G)
                    for b in range(NB):
                        cols = slice(b * SEQ, (b + 1) * SEQ)
                        mm = nc.tensor.transpose(p_s[:, cols], vT[:, cols], ident[:, :])
                    mm.then_inc(v_turned, 1)
                    query(1)
                    scores(0)
                    query(2)
                    scores(1)
                    values(0)
                    query(3)
                    scores(2)
                    values(1)
                    early = range(5)
                    pe.wait_ge(split_lo, base + C_WO)
                    pe.wait_ge(rot_mul, n * NR + NR)
                    out_part(early, 0)
                    scores(3)
                    values(2)
                    out_part(early, 1)
                    values(3)
                    out_part(early, 2)
                    out_part(early, 3)
                    for u in range(5, NU):
                        for h in range(G):
                            out_part([u], h)


def sign_ffn_stage(nc, x_in, gate, signW, bias, gate_wT, in_scale, out_scale, x_out):
    NE = 8
    with ExitStack() as ctx:
        def sb(name, shape, dt=F32):
            return ctx.enter_context(nc.sbuf_tensor("f_" + name, shape, dt))

        def ps(name, cols):
            return ctx.enter_context(nc.psum_tensor("fp_" + name, [P, cols], F32))

        def sem(name):
            return ctx.enter_context(nc.semaphore("f_" + name))

        w_raw = [sb(f"w_raw{i}", [P, DM]) for i in range(2)]
        w = sb("w", [P, KT, DM], F32R)
        gw = sb("gw", [P, KT, NE])
        ics = sb("ics", [NE, DM])
        ocs = sb("ocs", [NE, DM])
        tgb = sb("tgb", [P, DM])
        tg = sb("tg", [P, 1])
        ident = sb("ident", [P, P])
        eps = sb("eps", [P, 1])
        half_neg = sb("half_neg", [P, 1])
        x_sb = [sb(f"x{i}", [P, DM]) for i in range(4)]
        stats = sb("stats", [P, 2, 6])
        mv = sb("mv", [P, 2])
        rstd = sb("rstd", [P, 1])
        xn = [sb(f"xn{i}", [P, DM]) for i in range(2)]
        xnT = sb("xnT", [P, DM])
        small = sb("small", [P, 4])
        rt = sb("rt", [P, NE])
        rT = sb("rT", [NE, P])
        xs = sb("xs", [P, DM])
        xs_part = {(h, i): sb(f"xs_{h}{i}", [P, DM], F32R) for h in ("hi", "lo") for i in range(2)}
        osc = [sb(f"osc{i}", [P, DM]) for i in range(2)]
        xb = [sb(f"xb{i}", [P, DM]) for i in range(2)]
        y = sb("y", [P, DM])
        out_sb = [sb(f"out{i}", [P, DM]) for i in range(2)]

        p_t, p_o, p_y, p_l = ps("t", DM), ps("o", DM), ps("y", DM), ps("l", BANK)

        const_in = sem("const_in")
        const_pool = sem("const_pool")
        gate_done = sem("gate_done")
        w_in = [sem(f"w_in{i}") for i in range(2)]
        w_ready = sem("w_ready")
        x_in_s = [sem(f"x_in{i}") for i in range(4)]
        norm_steps = sem("norm_steps")
        stats_done = sem("stats_done")
        mv_done = sem("mv_done")
        var_done = sem("var_done")
        rstd_done = sem("rstd_done")
        xn_done = sem("xn_done")
        turned = sem("turned")
        xnT_out = sem("xnT_out")
        logits_done = sem("logits_done")
        max_done = sem("max_done")
        exp_done = sem("exp_done")
        rec_done = sem("rec_done")
        rt_done = sem("rt_done")
        rt_turned = sem("rt_turned")
        rT_out = sem("rT_out")
        in_scaled = sem("in_scaled")
        out_scaled = sem("out_scaled")
        xs_done = sem("xs_done")
        xs_hi = sem("xs_hi")
        xs_lo = sem("xs_lo")
        osc_out = sem("osc_out")
        xb_done = sem("xb_done")
        main_done = sem("main_done")
        y_done = sem("y_done")
        out_ready = sem("out_ready")
        out_store = [sem(f"out_store{i}") for i in range(2)]

        block = ctx.enter_context(nc.Block())

        def batch(view, i):
            return view[bass.ds(i, 1)].rearrange("o p n -> (o p) n")

        QUADS = BATCH // 4

        @block.sync
        def _(sp):
            sp.dma_start(gw[:, :, :], gate_wT.rearrange("(k p) e -> p k e", p=P)).then_inc(const_in, 16)
            sp.dma_start(ics[:, :], in_scale).then_inc(const_in, 16)
            sp.dma_start(ocs[:, :], out_scale).then_inc(const_in, 16)
            sp.dma_start(tgb[:, :], bias).then_inc(const_in, 16)
            sp.dma_start(tg[:, :], gate).then_inc(const_in, 16)
            for i in range(4):
                sp.dma_start(x_sb[i][:, :], x_in[i]).then_inc(x_in_s[i], 16)
            for k in range(KT):
                if k >= 2:
                    sp.wait_ge(w_ready, k - 1)
                sp.dma_start(w_raw[k % 2][:, :], signW[k * P:(k + 1) * P, :]).then_inc(w_in[k % 2], 16)

            def step(q, c, more):
                sp.wait_ge(out_ready, q * 4 + c + 1)
                sp.dma_start(batch(x_out, q * 4 + c), out_sb[c % 2][:, :]).then_inc(out_store[c % 2], 16)
                if more:
                    sp.wait_ge(xb_done, q * 4 + c + 1)
                    sp.dma_start(x_sb[c][:, :], batch(x_in, q * 4 + c + 4)).then_inc(x_in_s[c], 16)

            with sp.Fori(0, QUADS - 1) as q:
                for c in range(4):
                    step(q, c, True)
            for c in range(4):
                step(QUADS - 1, c, False)
            for i in range(2):
                sp.wait_ge(out_store[i], 16 * BATCH // 2)

        @block.gpsimd
        def _(pool):
            nc.gpsimd.memset(eps[:, :], EPS).then_inc(const_pool, 1)
            nc.gpsimd.memset(half_neg[:, :], -0.5).then_inc(const_pool, 1)
            nc.gpsimd.memset(ident[:, :], 0.0).then_inc(const_pool, 1)
            pool.wait_ge(const_pool, 3)
            nc.gpsimd.affine_select(out=ident[:, :], in_=ident[:, :], compare_op=ALU.not_equal, fill=1.0,
                                    base=0, pattern=[[-1, P]], channel_multiplier=1).then_inc(const_pool, 1)
            pool.wait_ge(gate_done, 1)
            pool.wait_ge(const_in, 80)
            nc.gpsimd.tensor_scalar(tgb[:, :], tgb[:, :], tg[:, 0:1], None, ALU.mult).then_inc(const_pool, 1)
            pool.wait_ge(const_pool, 5)

            def norm(q, c):
                b = q * 4 + c
                pool.wait_ge(mv_done, b + 1)
                pool.wait_ge(xn_done, b)
                nc.gpsimd.tensor_tensor(rstd[:, :], mv[:, 1:2], eps[:, :], ALU.add).then_inc(var_done, 1)
                pool.wait_ge(var_done, b + 1)
                nc.gpsimd.tensor_tensor(rstd[:, :], rstd[:, :], half_neg[:, :], ALU.pow).then_inc(rstd_done, 1)

            def scale(q, c):
                b, i = q * 4 + c, c % 2
                pool.wait_ge(xs_hi, b + 1)
                nc.gpsimd.tensor_tensor(xs_part["lo", i][:, :], xs[:, :], xs_part["hi", i][:, :].bitcast(F32),
                                        ALU.subtract).then_inc(xs_lo, 1)
                pool.wait_ge(x_in_s[c % 4], 16 * (q + c // 4) + 16)
                pool.wait_ge(out_ready, q * 4 + max(c - 1, 0))
                nc.gpsimd.tensor_tensor(xb[i][:, :], x_sb[c % 4][:, :], tgb[:, :], ALU.add).then_inc(xb_done, 1)

            def finish(q, c):
                b, i = q * 4 + c, c % 2
                pool.wait_ge(y_done, b + 1)
                pool.wait_ge(xb_done, b + 1)
                pool.wait_ge(out_store[i], (q * 2 + c // 2) * 16)
                nc.gpsimd.tensor_tensor(out_sb[i][:, :], y[:, :], xb[i][:, :], ALU.add).then_inc(out_ready, 1)

            norm(0, 0)
            norm(0, 1)
            scale(0, 0)

            def step(q, c, last):
                if not (last and c >= 2):
                    norm(q, c + 2)
                if not (last and c == 3):
                    scale(q, c + 1)
                finish(q, c)

            with pool.Fori(0, QUADS - 1) as q:
                for c in range(4):
                    step(q, c, False)
            for c in range(4):
                step(QUADS - 1, c, True)

        @block.scalar
        def _(act):
            act.wait_ge(const_in, 80)
            nc.scalar.activation(tg[:, :], tg[:, :], ACT.Tanh).then_inc(gate_done, 1)
            act.wait_ge(gate_done, 1)
            for k in range(KT):
                act.wait_ge(w_in[k % 2], 16 * (k // 2) + 16)
                nc.scalar.activation(w[:, k, :], w_raw[k % 2][:, :], ACT.Sign).then_inc(w_ready, 1)

            def route(q, c):
                b, i = q * 4 + c, c % 2
                act.wait_ge(turned, b + 1)
                act.wait_ge(xs_done, b)
                nc.scalar.activation(xnT[:, :], p_t[:, :], ACT.Copy).then_inc(xnT_out, 1)
                act.wait_ge(max_done, b + 1)
                act.wait_ge(rt_turned, b)
                nc.scalar.activation(rt[:, :], p_l[:, 0:NE], ACT.Exp, bias=small[:, 0:1],
                                     accum_out=small[:, 1:2]).then_inc(exp_done, 1)
                act.wait_ge(out_scaled, b + 1)
                act.wait_ge(y_done, q * 4 + max(c - 1, 0))
                nc.scalar.activation(osc[i][:, :], p_o[:, :], ACT.Identity, scale=tg[:, 0:1]).then_inc(osc_out, 1)
                act.wait_ge(xs_done, b + 1)
                act.wait_ge(main_done, q * 4 + max(c - 1, 0))
                nc.scalar.activation(xs_part["hi", i][:, :], xs[:, :], ACT.Copy).then_inc(xs_hi, 1)

            route(0, 0)

            def step(q, c, last):
                if not (last and c == 3):
                    route(q, c + 1)

            with act.Fori(0, QUADS - 1) as q:
                for c in range(4):
                    step(q, c, False)
            for c in range(4):
                step(QUADS - 1, c, True)

        @block.vector
        def _(dve):
            def norm(q, c):
                b, i = q * 4 + c, c % 2
                x = x_sb[c % 4]
                dve.wait_ge(x_in_s[c % 4], 16 * (q + c // 4) + 16)
                dve.wait_ge(mv_done, b)
                for h in range(2):
                    nc.vector.bn_stats(stats[:, h, :], x[:, h * BANK:(h + 1) * BANK]).then_inc(stats_done, 1)
                dve.wait_ge(stats_done, 2 * b + 2)
                dve.wait_ge(rstd_done, b)
                dve.sem_inc(norm_steps, 1)
                nc.vector.bn_aggr(mv[:, :], stats[:, :, :]).then_inc(mv_done, 1)
                dve.wait_ge(rstd_done, b + 1)
                dve.wait_ge(turned, q * 4 + max(c - 1, 0))
                nc.vector.tensor_scalar(xn[i][:, :], x[:, :], mv[:, 0:1], rstd[:, 0:1], ALU.subtract, ALU.mult)\
                    .then_inc(xn_done, 1)

            def route(q, c):
                b = q * 4 + c
                dve.wait_ge(logits_done, b + 1)
                dve.wait_ge(rt_done, b)
                nc.vector.tensor_reduce(small[:, 0:1], p_l[:, 0:NE], AX.X, ALU.max, negate=True)\
                    .then_inc(max_done, 1)
                dve.wait_ge(exp_done, b + 1)
                nc.vector.reciprocal(small[:, 2:3], small[:, 1:2]).then_inc(rec_done, 1)
                dve.wait_ge(rec_done, b + 1)
                nc.vector.tensor_scalar(rt[:, :], rt[:, :], small[:, 2:3], None, ALU.mult).then_inc(rt_done, 1)
                dve.wait_ge(rt_turned, b + 1)
                nc.vector.tensor_copy(rT[:, :], p_l[0:NE, P:2 * P]).then_inc(rT_out, 1)

            def scale(q, c):
                b = q * 4 + c
                dve.wait_ge(in_scaled, b + 1)
                dve.wait_ge(xs_lo, b)
                nc.vector.tensor_tensor(xs[:, :], p_t[:, :], xnT[:, :], ALU.mult).then_inc(xs_done, 1)

            def finish(q, c):
                b, i = q * 4 + c, c % 2
                dve.wait_ge(main_done, b + 1)
                dve.wait_ge(osc_out, b + 1)
                dve.wait_ge(out_ready, b)
                nc.vector.tensor_tensor(y[:, :], p_y[:, :], osc[i][:, :], ALU.mult).then_inc(y_done, 1)

            norm(0, 0)
            norm(0, 1)
            route(0, 0)
            scale(0, 0)

            def step(q, c, last):
                if not (last and c == 3):
                    route(q, c + 1)
                if not (last and c >= 2):
                    norm(q, c + 2)
                if not (last and c == 3):
                    scale(q, c + 1)
                finish(q, c)

            with dve.Fori(0, QUADS - 1) as q:
                for c in range(4):
                    step(q, c, False)
            for c in range(4):
                step(QUADS - 1, c, True)

        @block.tensor
        def _(pe):
            def turn(q, c):
                b = q * 4 + c
                pe.wait_ge(xn_done, b + 1)
                pe.wait_ge(xs_done, b)
                for k in range(KT):
                    mm = nc.tensor.transpose(p_t[:, k * P:(k + 1) * P], xn[c % 2][:, k * P:(k + 1) * P], ident[:, :])
                mm.then_inc(turned, 1)

            def logits(q, c):
                b = q * 4 + c
                pe.wait_ge(xnT_out, b + 1)
                pe.wait_ge(rT_out, b)
                for k in range(KT):
                    mm = nc.tensor.matmul(p_l[:, 0:NE], xnT[:, k * P:(k + 1) * P], gw[:, k, :],
                                          start=(k == 0), stop=(k == KT - 1))
                mm.then_inc(logits_done, 1)

            def turn_routing(q, c):
                b = q * 4 + c
                pe.wait_ge(rt_done, b + 1)
                nc.tensor.transpose(p_l[0:NE, P:2 * P], rt[:, :], ident[:, :]).then_inc(rt_turned, 1)

            def scales(q, c):
                b = q * 4 + c
                pe.wait_ge(rT_out, b + 1)
                for k in range(KT):
                    mm = nc.tensor.matmul(p_t[:, k * P:(k + 1) * P], ics[:, k * P:(k + 1) * P], rT[:, :],
                                          start=True, stop=True)
                mm.then_inc(in_scaled, 1)
                pe.wait_ge(osc_out, b)
                for h in range(2):
                    mm = nc.tensor.matmul(p_o[:, h * BANK:(h + 1) * BANK], rT[:, :], ocs[:, h * BANK:(h + 1) * BANK],
                                          start=True, stop=True)
                mm.then_inc(out_scaled, 1)

            def main(q, c, part):
                b = q * 4 + c
                if part == 0:
                    pe.wait_ge(xs_lo, b + 1)
                    pe.wait_ge(y_done, b)
                for k in range(2 * part, 2 * part + 2):
                    for h in range(2):
                        for n, t in enumerate(("hi", "lo")):
                            mm = nc.tensor.matmul(p_y[:, h * BANK:(h + 1) * BANK],
                                                  xs_part[t, c % 2][:, k * P:(k + 1) * P],
                                                  w[:, k, h * BANK:(h + 1) * BANK],
                                                  start=(k == 0 and n == 0), stop=(k == KT - 1 and n == 1))
                if part == 3:
                    mm.then_inc(main_done, 1)

            pe.wait_ge(const_pool, 5)
            pe.wait_ge(const_in, 80)
            turn(0, 0)
            logits(0, 0)
            turn_routing(0, 0)
            scales(0, 0)
            pe.wait_ge(w_ready, KT)

            def step(q, c, last):
                ahead = not (last and c == 3)
                if ahead:
                    turn(q, c + 1)
                main(q, c, 0)
                if ahead:
                    logits(q, c + 1)
                main(q, c, 1)
                if ahead:
                    turn_routing(q, c + 1)
                main(q, c, 2)
                if ahead:
                    scales(q, c + 1)
                main(q, c, 3)

            with pe.Fori(0, QUADS - 1) as q:
                for c in range(4):
                    step(q, c, False)
            for c in range(4):
                step(QUADS - 1, c, True)


def flamingo_layers(nc, a, out):
    def scratch(name, shape):
        return nc.dram_tensor(name, shape, F32, kind="Internal").ap()

    x2 = scratch("x_after_layer0", (BATCH, SEQ, DM))
    x3 = scratch("x_after_attention", (BATCH, SEQ, DM))
    xnT = scratch("xn_turned", (BATCH, P, KT, SEQ))
    ctxT = scratch("ctx_turned", (BATCH, P, KT, SEQ))
    linear_attention_moe_stage(nc, a["x"], a["ctx"], a["L0_WqT"], a["L0_WkT"], a["L0_Wv"], a["L0_WoT"], a["L0_bo"],
                               a["L0_g"], a["gate_x0"], a["gate_f0"], a["L0_WbT"], a["L0_bias"], a["L0_AT"],
                               a["L0_WrT"], a["L0_BmT"], a["prio"], x2, xnT, ctxT)
    gqa_stage(nc, x2, xnT, ctxT, a["mask"], a["gate_x1"], a["L1_Wq"], a["L1_Wk"], a["L1_Wv"], a["L1_Wo"],
              a["cos"], a["sin"], x3)
    sign_ffn_stage(nc, x3, a["gate_f1"], a["L1_signT"], a["L1_bias"], a["L1_gateT"], a["L1_in_scale"],
                   a["L1_out_scale"], out)


def rotary_tables(seq, d):
    inv_freq = (1.0 / 10000.0 ** (np.arange(0, d, 2, dtype=np.float32) / np.float32(d))).astype(np.float32)
    phase = inv_freq[:, None] * np.arange(seq, dtype=np.float32)[None, :]
    cos, sin = np.cos(phase), np.sin(phase)
    return np.concatenate([cos, cos]), np.concatenate([sin, -sin])


def kernel(**inputs):
    import concourse.bacc as _bacc
    from concourse.bass_utils import run_bass_kernel_spmd as _run

    v = {k: np.asarray(x) for k, x in inputs.items()}

    def rows(t):
        return np.broadcast_to(t.reshape(1, -1), (P, t.size))

    cos, sin = rotary_tables(SEQ, P)
    laid_out = {
        "x": v["x"], "ctx": v["ctx_4096"],
        "mask": v["mask_1x1xSxS2_bk0"].reshape(SEQ, SEQ).view(np.uint32),
        "gate_x0": rows(v["g_xattn"][0:1]), "gate_x1": rows(v["g_xattn"][1:2]),
        "gate_f0": rows(v["g_ffn"][0:1]), "gate_f1": rows(v["g_ffn"][1:2]),
        "L0_WqT": v["L0_xattn_Wq"].T, "L0_WkT": v["L0_xattn_Wk"].T, "L0_Wv": v["L0_xattn_Wv"],
        "L0_WoT": v["L0_xattn_Wo"].T, "L0_bo": v["L0_xattn_bo"].reshape(P, 1), "L0_g": v["L0_xattn_g"].reshape(P, 1),
        "L0_WbT": v["L0_ffn_Wb"].T, "L0_bias": rows(v["L0_ffn_bias"]),
        "L0_AT": v["L0_ffn_A"].reshape(-1, DM).T, "L0_WrT": v["L0_ffn_Wr"].T,
        "L0_BmT": v["L0_ffn_Bm"].transpose(0, 2, 1).reshape(-1, DM),
        "prio": rows(np.arange(8, 0, -1, dtype=np.float32)),
        "L1_Wq": v["L1_xattn_Wq"], "L1_Wk": v["L1_xattn_Wk"], "L1_Wv": v["L1_xattn_Wv"], "L1_Wo": v["L1_xattn_Wo"],
        "cos": cos, "sin": sin,
        "L1_signT": v["L1_ffn_weight"].T, "L1_bias": rows(v["L1_ffn_bias"]), "L1_gateT": v["L1_ffn_gate_w"].T,
        "L1_in_scale": v["L1_ffn_in_channel_scale"], "L1_out_scale": v["L1_ffn_out_channel_scale"],
    }
    nc = _bacc.Bacc("TRN2", target_bir_lowering=False, num_devices=1)
    arrays, args = {}, {}
    for name, a in laid_out.items():
        a = np.ascontiguousarray(a)
        arrays[f"in_{name}"] = a
        args[name] = nc.dram_tensor(f"in_{name}", a.shape, mybir.dt.from_np(a.dtype), kind="ExternalInput").ap()
    out = nc.dram_tensor("out_x", (BATCH, SEQ, DM), F32, kind="ExternalOutput").ap()
    flamingo_layers(nc, args, out)
    r = _run(nc, [arrays], core_ids=[0])
    return r.results[0]["out_x"]
```

```python
from contextlib import ExitStack
import math

import numpy as np
import concourse.bass as bass
from concourse import mybir

F32 = mybir.dt.float32
F32R = mybir.dt.float32r
U8 = mybir.dt.uint8
U32 = mybir.dt.uint32
ALU = mybir.AluOpType
ACT = mybir.ActivationFunctionType
AX = mybir.AxisListType

P = 128
BANK = 512
FIRST = 1
BATCH, SEQ, DM = 16, 128, 1024
KT = DM // P
EPS = 1e-5
SPLIT = (("hi", "hi"), ("hi", "lo"), ("lo", "hi"))


def linear_attention_moe_stage(nc, x_in, c_in, WqT, WkT, Wv, WoT, bo, g_norm, gate_x, gate_f, WbT, bias, AT, WrT,
                               BmT, prio, x_out, xnT_out, ctxT_out):
    H, DH = 8, 64
    HID = H * DH
    MT = HID // P
    NE, R = 8, 16
    ER = NE * R

    with ExitStack() as ctx:
        def sb(name, shape, dt=F32):
            return ctx.enter_context(nc.sbuf_tensor("a_" + name, shape, dt))

        def ps(name, cols):
            return ctx.enter_context(nc.psum_tensor("ap_" + name, [P, cols], F32))

        def sem(name):
            return ctx.enter_context(nc.semaphore("a_" + name))

        def pair(name, shape):
            return {h: sb(f"{name}_{h}", shape, F32R) for h in ("hi", "lo")}

        wq, wk = pair("wq", [P, HID]), pair("wk", [P, HID])
        wb = pair("wb", [P, KT, DM])
        avo = sb("avo", [P, H, P])
        ar = sb("ar", [P, KT, ER + NE])
        bm = sb("bm", [ER, DM])
        ident, ones = sb("ident", [P, P]), sb("ones", [P, P])
        prio_sb = sb("prio", [P, NE])
        half_neg = sb("half_neg", [P, KT])
        eps = sb("eps", [P, 1])
        bo_sb, sc, tgf = sb("bo", [P, 1]), sb("sc", [P, 1]), sb("tgf", [P, 1])
        tgx, gn = sb("tgx", [P, 1]), sb("gn", [P, 1])
        tgb = sb("tgb", [P, DM])
        x_sb = [sb(f"xin{i}", [P, DM]) for i in range(2)]
        c_sb = [sb(f"c{i}", [P, DM]) for i in range(2)]
        xn_f = sb("xn_f", [P, DM])
        xn, cc = pair("xn", [P, DM]), pair("cc", [P, DM])
        cT = sb("cT", [P, KT, P])
        ke = sb("ke", [P, MT, DM])
        kneg, ksum, krec = sb("kneg", [P, MT]), sb("ksum", [P, MT]), sb("krec", [P, MT])
        qs = [sb(f"qs{i}", [P, HID]) for i in range(4)]
        qmax, qsum = sb("qmax", [P, H]), sb("qsum", [P, H])
        qrec = [sb(f"qrec{i}", [P, H]) for i in range(2)]
        qT = sb("qT", [P, MT, DM])
        keT, g_sb = qs[1:3], qs[0]
        w2 = sb("w2", [P, MT, P])
        o_sb = sb("o_sb", [P, DM])
        ss, rn = sb("ss", [P, KT]), sb("rn", [P, KT])
        t_sb = sb("t_sb", [P, DM])
        x1, x1b = sb("x1", [P, DM]), sb("x1b", [P, DM])
        sq = x1
        hT = sb("hT", [ER, P])
        xT_f = xn_f[:, :].rearrange("p (k t) -> p k t", k=KT)
        xT = pair("xT", [P, KT, P])
        h_sb = sb("h_sb", [P, ER])
        ex, rt, sel, tmp = (sb(n, [P, NE]) for n in ("ex", "rt", "sel", "tmp"))
        sm = sb("sm", [P, 8])
        x2 = sb("x2", [P, DM])
        x2T = sb("x2T", [P, KT, P])
        diag = x2T
        ln = {n: (sb(f"st_{n}", [P, 2, 6]), sb(f"mv_{n}", [P, 2]), sb(f"rs_{n}", [P, 1])) for n in ("x", "1", "2")}
        raw = [t_sb, x1, x1b, x2]

        p_k = ps("k", DM)
        p_tr = [ps("t0", BANK), ps("t1", BANK)]
        p_q = ps("q", BANK)
        p_y = ps("y", DM)
        p_g = ps("g", BANK)

        names = """k_used const_in const_pool const_act w_hi w_lo avo_done in_hi in_lo tr_done tr_out k_proj kmax_done kexp krec_done q_proj qmax_done qsub qexp
            qsum_done qrec_done qnorm g_out w2_done w2_out out_done o_out sq_done
            ss_done ss_out ss_pow diag_done spread_done t_done x1_done x1b_done xT_hi xT_lo lora_done
            route_max route_exp route_step h_done h_turned hT_out y_done x2_done ctxT_st xnT_st x2_st
            ctxT_free xnT_free x2_free"""
        S = {n: sem(n) for n in names.split()}
        w_land = [sem(f"w_land{i}") for i in range(4)]
        x_land = [sem(f"x_land{i}") for i in range(2)]
        c_land = [sem(f"c_land{i}") for i in range(2)]
        LN = {n: {k: sem(f"ln_{n}_{k}") for k in ("moments", "rstd", "done")} for n in ("x", "1", "2")}

        ATT_UNITS = [("ctx", 0), ("ctx", 1)] + [("q", r) for r in range(KT)] + [("k", r) for r in range(KT)]
        FULL_UNITS = ([("ctx", 0), ("ctx", 1), ("q", 0), ("q", 1), ("q", 2), ("x", 0), ("x", 1)]
                      + [("q", r) for r in range(3, KT)] + [("k", r) for r in range(6)]
                      + [("n", 0), ("n", 1), ("k", 6), ("k", 7)])
        FFN_UNITS = [("x", 0), ("x", 1), ("n", 0), ("n", 1)]
        W_CHUNKS = KT + 2

        class Step:

            def __init__(self, s0, c, att, ffn, half):
                self.s, self.c, self.att, self.ffn = s0 + c, c, att, ffn
                self.par, self.half = c % 2, half
                self.units = FULL_UNITS if att and ffn else ATT_UNITS if att else FFN_UNITS
                self.tr0 = (s0 + (c - 1)) * len(FULL_UNITS) + len(ATT_UNITS) if ffn else 0
                self.fresh = not ffn

            def at(self, n, k):
                return self.s * n + k

            def before(self, n, k):
                return (self.s - 1) * n + k

            def unit(self, name):
                return self.tr0 + self.units.index(name)

        def steps(engine, body):
            body(Step(0, 0, True, False, 0))
            pairs = (BATCH - 2) // 2
            with engine.Fori(0, pairs) as t:
                body(Step(2 * t, 1, True, True, t))
                body(Step(2 * t, 2, True, True, t + 1))
            body(Step(0, BATCH - 1, True, True, BATCH // 2 - 1))
            body(Step(0, BATCH, False, True, BATCH // 2))

        block = ctx.enter_context(nc.Block())

        def batch(view, i):
            return view[bass.ds(i, 1)].rearrange("o p n -> (o p) n") if not isinstance(i, int) else view[i]

        def tview(view, s):
            return view[bass.ds(s, 1)].rearrange("o p k t -> (o p) k t") if not isinstance(s, int) else view[s]

        def heads(t):
            return t.rearrange("p (h d) -> p h d", h=H)

        def spread(t, n):
            return t.rearrange("p (m o) -> p m o", o=1).to_broadcast([P, t.shape[-1], n])

        @block.sync
        def _(sp):
            for name in ("ctxT_free", "xnT_free", "x2_free"):
                sp.sem_inc(S[name], 1)
            small = ((bo_sb, bo), (gn, g_norm), (tgx, gate_x), (tgf, gate_f), (tgb, bias), (prio_sb, prio),
                     (bm, BmT), (ar[:, :, 0:ER], AT.rearrange("(k p) n -> p k n", p=P)),
                     (ar[:, :, ER:ER + NE], WrT.rearrange("(k p) n -> p k n", p=P)),
                     (ke[0:DH, 0, :].rearrange("e (h c) -> e h c", h=H), Wv.rearrange("(h e) c -> e h c", e=DH)),
                     (ke[0:DH, 1, :].rearrange("e (h c) -> e h c", h=H), WoT.rearrange("(h e) c -> e h c", e=DH)))
            for dst, src in small:
                sp.dma_start(dst if isinstance(dst, bass.AP) else dst[:, :], src).then_inc(S["const_in"], 16)
            for i in range(W_CHUNKS):
                if i >= 4:
                    sp.wait_ge(S["w_lo"], FIRST + i - 3)
                src = (WqT, WkT)[i] if i < 2 else WbT[(i - 2) * P:(i - 1) * P, :]
                sp.dma_start(raw[i % 4][:, 0:src.shape[1]], src).then_inc(w_land[i % 4], 16)
                if i < 2:
                    sp.dma_start(c_sb[i][:, :], c_in[i]).then_inc(c_land[i], 16)
                    sp.dma_start(x_sb[i][:, :], x_in[i]).then_inc(x_land[i], 16)

            def body(z):
                if z.att:
                    sp.wait_ge(S["tr_out"], FIRST + z.unit(("ctx", 1)) + 1)
                    sp.dma_start(tview(ctxT_out, z.s), cT[:, :, :]).then_inc(S["ctxT_st"], 16)
                if z.ffn and z.c != BATCH - 1 and z.c != BATCH:
                    sp.wait_ge(S["x1_done"], FIRST + z.s)
                    sp.dma_start(x_sb[1 - z.par][:, :], batch(x_in, z.s + 1)).then_inc(x_land[1 - z.par], 16)
                    sp.dma_start(c_sb[1 - z.par][:, :], batch(c_in, z.s + 1)).then_inc(c_land[1 - z.par], 16)
                if z.ffn:
                    sp.wait_ge(S["x2_done"], FIRST + z.s)
                    sp.dma_start(batch(x_out, z.s - 1), x2[:, :]).then_inc(S["x2_st"], 16)
                if z.att:
                    sp.wait_ge(S["ctxT_st"], z.s * 16 + 16)
                    sp.sem_inc(S["ctxT_free"], 1)
                if z.ffn:
                    sp.wait_ge(S["tr_out"], FIRST + z.unit(("n", 1)) + 1)
                    sp.dma_start(tview(xnT_out, z.s - 1), x2T[:, :, :]).then_inc(S["xnT_st"], 16)
                    sp.wait_ge(S["x2_st"], z.s * 16)
                    sp.sem_inc(S["x2_free"], 1)
                    sp.wait_ge(S["xnT_st"], z.s * 16)
                    sp.sem_inc(S["xnT_free"], 1)

            steps(sp, body)
            for n in ("ctxT_st", "x2_st", "xnT_st"):
                sp.wait_ge(S[n], 16 * BATCH)

        @block.gpsimd
        def _(pool):
            for name in ("const_pool", "w_lo", "in_lo", "qnorm", "ss_pow",
                         "diag_done", "x1_done", "x1b_done", "xT_lo", "sq_done"):
                pool.sem_inc(S[name], 1)
            for n in LN:
                pool.sem_inc(LN[n]["rstd"], 1)
            def lo(part, src, view=lambda t: t):
                return nc.gpsimd.tensor_tensor(view(part["lo"][:, :]), src, view(part["hi"][:, :]).bitcast(F32),
                                               ALU.subtract)

            nc.gpsimd.memset(eps[:, :], EPS).then_inc(S["const_pool"], 1)
            nc.gpsimd.memset(half_neg[:, :], -0.5).then_inc(S["const_pool"], 1)
            nc.gpsimd.memset(ones[:, :], 1.0).then_inc(S["const_pool"], 1)
            nc.gpsimd.memset(ident[:, :], 0.0).then_inc(S["const_pool"], 1)
            pool.wait_ge(S["const_pool"], FIRST + 4)
            nc.gpsimd.affine_select(out=ident[:, :], in_=ident[:, :], compare_op=ALU.not_equal, fill=1.0,
                                    base=0, pattern=[[-1, P]], channel_multiplier=1).then_inc(S["const_pool"], 1)
            pool.wait_ge(S["const_in"], 16 * 11)
            pool.wait_ge(S["const_act"], FIRST + 2)
            nc.gpsimd.tensor_scalar(tgb[:, :], tgb[:, :], tgf[:, 0:1], None, ALU.mult).then_inc(S["const_pool"], 1)
            nc.gpsimd.tensor_scalar(sc[:, :], tgx[:, :], gn[:, 0:1], math.sqrt(SEQ), ALU.mult, ALU.mult)\
                .then_inc(S["const_pool"], 1)
            for i in range(W_CHUNKS):
                pool.wait_ge(S["w_hi"], FIRST + i + 1)
                if i < 2:
                    lo((wq, wk)[i], raw[i][:, 0:HID]).then_inc(S["w_lo"], 1)
                else:
                    nc.gpsimd.tensor_tensor(wb["lo"][:, i - 2, :], raw[i % 4][:, :],
                                            wb["hi"][:, i - 2, :].bitcast(F32), ALU.subtract).then_inc(S["w_lo"], 1)
            pool.wait_ge(S["const_pool"], FIRST + 7)

            def rstd(n, b):
                st, mv, rs = ln[n]
                sems = LN[n]
                pool.wait_ge(sems["moments"], FIRST + 4 * b + 4)
                pool.wait_ge(sems["done"], FIRST + b)
                nc.gpsimd.tensor_tensor(rs[:, :], mv[:, 1:2], eps[:, :], ALU.add).then_inc(sems["rstd"], 1)
                pool.wait_ge(sems["rstd"], FIRST + 2 * b + 1)
                nc.gpsimd.tensor_tensor(rs[:, :], rs[:, :], half_neg[:, 0:1], ALU.pow).then_inc(sems["rstd"], 1)

            def prepare(b, par):
                rstd("x", b)
                pool.wait_ge(S["in_hi"], FIRST + 2 * b + 1)
                lo(cc, c_sb[par][:, :]).then_inc(S["in_lo"], 1)
                pool.wait_ge(S["in_hi"], FIRST + 2 * b + 2)
                lo(xn, xn_f[:, :]).then_inc(S["in_lo"], 1)

            prepare(0, 0)

            def body(z):
                s = z.s

                def q_norm(r):
                    pool.wait_ge(S["qrec_done"], FIRST + z.at(KT, r + 1))
                    nc.gpsimd.tensor_tensor(heads(qs[r % 4][:, :]), heads(qs[r % 4][:, :]), spread(qrec[r % 2][:, :], DH),
                                            ALU.mult).then_inc(S["qnorm"], 1)

                if z.ffn:
                    pool.wait_ge(S["ss_out"], FIRST + s)
                    nc.gpsimd.tensor_tensor(rn[:, :], ss[:, :], half_neg[:, :], ALU.pow).then_inc(S["ss_pow"], 1)
                    pool.wait_ge(S["ss_pow"], FIRST + s)
                    pool.wait_ge(S["xnT_free"], FIRST + s - 1)
                    nc.gpsimd.tensor_tensor(diag[:, :, :], ident[:, :].rearrange("p (o n) -> p o n", o=1)
                                            .to_broadcast([P, KT, P]), spread(rn[:, :], P), ALU.mult)\
                        .then_inc(S["diag_done"], 1)
                if z.att:
                    q_norm(0)
                if z.ffn:
                    pool.wait_ge(S["t_done"], FIRST + s)
                    nc.gpsimd.tensor_tensor(x1[:, :], x_sb[1 - z.par][:, :], t_sb[:, :], ALU.add)\
                        .then_inc(S["x1_done"], 1)
                if z.att:
                    q_norm(1)
                if z.ffn:
                    rstd("1", s - 1)
                if z.att:
                    q_norm(2)
                if z.ffn:
                    pool.wait_ge(S["x1_done"], FIRST + s)
                    nc.gpsimd.tensor_tensor(x1b[:, :], x1[:, :], tgb[:, :], ALU.add).then_inc(S["x1b_done"], 1)
                if z.att:
                    q_norm(3)
                    q_norm(4)
                if z.ffn:
                    pool.wait_ge(S["xT_hi"], FIRST + s)
                    nc.gpsimd.tensor_tensor(xT["lo"][:, :, :], xT_f[:, :, :], xT["hi"][:, :, :].bitcast(F32),
                                            ALU.subtract).then_inc(S["xT_lo"], 1)
                if z.att:
                    for r in range(5, KT):
                        q_norm(r)
                if z.ffn:
                    rstd("2", s - 1)
                if z.att and z.c != BATCH - 1:
                    prepare(s + 1, 1 - z.par)
                if z.att:
                    pool.wait_ge(S["o_out"], FIRST + s + 1)
                    pool.wait_ge(LN["1"]["done"], FIRST + s)
                    nc.gpsimd.tensor_tensor(sq[:, :], o_sb[:, :], o_sb[:, :], ALU.mult).then_inc(S["sq_done"], 1)

            steps(pool, body)

        @block.scalar
        def _(act):
            for name in ("const_act", "w_hi", "in_hi", "tr_out", "kexp", "qexp", "xT_hi",
                         "route_exp", "g_out", "o_out"):
                act.sem_inc(S[name], 1)
            A = nc.scalar.activation
            act.wait_ge(S["const_in"], 16 * 11)
            A(tgx[:, :], tgx[:, :], ACT.Tanh).then_inc(S["const_act"], 1)
            A(tgf[:, :], tgf[:, :], ACT.Tanh).then_inc(S["const_act"], 1)
            act.wait_ge(S["avo_done"], FIRST + 1)
            A(avo[:, :, :], p_k[:, :].rearrange("p (h o) -> p h o", h=H), ACT.Copy).then_inc(S["const_act"], 1)
            for i in range(W_CHUNKS):
                act.wait_ge(w_land[i % 4], 16 * (i // 4) + 16)
                if i < 2:
                    A((wq, wk)[i]["hi"][:, :], raw[i][:, 0:HID], ACT.Copy).then_inc(S["w_hi"], 1)
                else:
                    A(wb["hi"][:, i - 2, :], raw[i % 4][:, :], ACT.Copy).then_inc(S["w_hi"], 1)
            act.wait_ge(S["const_pool"], FIRST + 7)

            def prepare(b, par, half):
                act.wait_ge(c_land[par], 16 * half + 16)
                act.wait_ge(S["k_proj"], FIRST + b * MT)
                A(cc["hi"][:, :], c_sb[par][:, :], ACT.Copy).then_inc(S["in_hi"], 1)
                act.wait_ge(LN["x"]["done"], FIRST + b + 1)
                act.wait_ge(S["q_proj"], FIRST + b * KT)
                A(xn["hi"][:, :], xn_f[:, :], ACT.Copy).then_inc(S["in_hi"], 1)

            prepare(0, 0, 0)

            def body(z):
                s = z.s

                def copy_out(name):
                    kind, r = name
                    u = z.unit(name)
                    src = p_tr[u % 2 if isinstance(u, int) else z.units.index(name) % 2]
                    t3 = src[:, :].rearrange("p (k n) -> p k n", k=4)
                    dst = {"ctx": lambda: cT[:, 4 * r:4 * r + 4, :],
                           "q": lambda: qT[:, :, r * P:(r + 1) * P],
                           "k": lambda: keT[r % 2][:, :].rearrange("p (k n) -> p k n", k=4),
                           "x": lambda: xT_f[:, 4 * r:4 * r + 4, :],
                           "n": lambda: x2T[:, 4 * r:4 * r + 4, :]}[kind]()
                    act.wait_ge(S["tr_done"], FIRST + u + 1)
                    A(dst, t3, ACT.Copy).then_inc(S["tr_out"], 1)

                def k_exp(m):
                    act.wait_ge(S["kmax_done"], FIRST + z.at(MT, m + 1))
                    A(ke[:, m, :], p_k[:, :], ACT.Exp, bias=kneg[:, m:m + 1], accum_out=ksum[:, m:m + 1])\
                        .then_inc(S["kexp"], 1)

                def q_exp(r):
                    act.wait_ge(S["qsub"], FIRST + z.at(KT, r + 1))
                    A(qs[r % 4][:, :], qs[r % 4][:, :], ACT.Exp).then_inc(S["qexp"], 1)

                if z.att:
                    act.wait_ge(S["ctxT_free"], FIRST + s)
                    act.wait_ge(S["k_used"], FIRST + z.at(KT, 0))
                    copy_out(("ctx", 0))
                    copy_out(("ctx", 1))
                    act.wait_ge(S["w2_out"], FIRST + s)
                for r in range(KT):
                    if z.att:
                        if r % 2 == 0:
                            k_exp(r // 2)
                        q_exp(r)
                        if r == 2:
                            act.wait_ge(S["out_done"], FIRST + s)
                        if r >= 2:
                            copy_out(("q", r - 2))
                    if z.ffn and r == 4:
                        act.wait_ge(S["lora_done"], FIRST + s - 1)
                        act.wait_ge(S["xT_lo"], FIRST + s - 1)
                        act.wait_ge(S["in_lo"], FIRST + (z.at(2, 2) if z.att else 2 * s))
                        copy_out(("x", 0))
                        copy_out(("x", 1))
                        act.wait_ge(S["tr_out"], FIRST + z.unit(("x", 1)) + 1)
                        act.wait_ge(S["y_done"], FIRST + s - 1)
                        A(xT["hi"][:, :, :], xT_f[:, :, :], ACT.Copy).then_inc(S["xT_hi"], 1)
                    if z.ffn and r == 5:
                        act.wait_ge(S["route_max"], FIRST + s)
                        A(ex[:, :], p_g[:, ER:ER + NE], ACT.Exp, bias=sm[:, 0:1]).then_inc(S["route_exp"], 1)
                if z.att:
                    copy_out(("q", KT - 2))
                    copy_out(("q", KT - 1))
                    for r in range(6):
                        act.wait_ge(S["k_used"], FIRST + z.at(KT, max(r - 1, 0)))
                        copy_out(("k", r))
                if z.ffn:
                    act.wait_ge(S["xnT_free"], FIRST + s - 1)
                    copy_out(("n", 0))
                    copy_out(("n", 1))
                if z.att:
                    for r in range(6, KT):
                        act.wait_ge(S["k_used"], FIRST + z.at(KT, r - 1))
                        copy_out(("k", r))
                    if z.c != BATCH - 1:
                        prepare(s + 1, 1 - z.par, z.half + (1 if z.par else 0))
                    act.wait_ge(S["k_used"], FIRST + z.at(KT, KT))
                    A(g_sb[:, :], p_g[:, :], ACT.Copy).then_inc(S["g_out"], 1)
                    act.wait_ge(S["out_done"], FIRST + s + 1)
                    act.wait_ge(S["t_done"], FIRST + s)
                    act.wait_ge(S["sq_done"], FIRST + s)
                    A(o_sb[:, :], p_k[:, :], ACT.Identity, bias=bo_sb[:, 0:1]).then_inc(S["o_out"], 1)

            steps(act, body)

        @block.vector
        def _(dve):
            for name in ("kmax_done", "qmax_done", "qsub", "qsum_done", "qrec_done", "ss_out", "t_done",
                         "route_max", "route_step", "h_done", "hT_out", "krec_done", "x2_done", "w2_out"):
                dve.sem_inc(S[name], 1)
            for n in LN:
                for k in ("moments", "done"):
                    dve.sem_inc(LN[n][k], 1)
            V = nc.vector

            def norm(n, src, dst, b, free):
                st, mv, rs = ln[n]
                sems = LN[n]
                dve.wait_ge(sems["moments"], FIRST + 4 * b)
                for h in range(2):
                    V.bn_stats(st[:, h, :], src[:, h * BANK:(h + 1) * BANK]).then_inc(sems["moments"], 1)
                dve.wait_ge(sems["moments"], FIRST + 4 * b + 2)
                dve.wait_ge(sems["done"], FIRST + b)
                dve.sem_inc(sems["moments"], 1)
                V.bn_aggr(mv[:, :], st[:, :, :]).then_inc(sems["moments"], 1)

            def norm_apply(n, src, dst, b):
                st, mv, rs = ln[n]
                dve.wait_ge(LN[n]["rstd"], FIRST + 2 * b + 2)
                V.tensor_scalar(dst[:, :], src[:, :], mv[:, 0:1], rs[:, 0:1], ALU.subtract, ALU.mult)\
                    .then_inc(LN[n]["done"], 1)

            def prepare(b, par, half):
                dve.wait_ge(x_land[par], 16 * half + 16)
                norm("x", x_sb[par], xn_f, b, None)

            def prepare_apply(b, par, ffn=0):
                dve.wait_ge(S["in_lo"], FIRST + 2 * b)
                if not isinstance(ffn, int) or ffn > 0:
                    dve.wait_ge(S["xT_lo"], FIRST + ffn)
                    dve.wait_ge(S["lora_done"], FIRST + ffn)
                norm_apply("x", x_sb[par], xn_f, b)

            prepare(0, 0, 0)
            prepare_apply(0, 0)

            def body(z):
                s = z.s

                def k_max(m):
                    dve.wait_ge(S["k_proj"], FIRST + z.at(MT, m + 1))
                    dve.wait_ge(S["kexp"], FIRST + z.at(MT, m))
                    V.tensor_reduce(kneg[:, m:m + 1], p_k[:, :], AX.X, ALU.max, negate=True)\
                        .then_inc(S["kmax_done"], 1)

                def q_shift(r):
                    dve.wait_ge(S["q_proj"], FIRST + z.at(KT, r + 1))
                    dve.wait_ge(S["qsub"], FIRST + z.at(KT, r))
                    V.tensor_reduce(qmax[:, :], heads(p_q[:, :]), AX.X, ALU.max).then_inc(S["qmax_done"], 1)
                    dve.wait_ge(S["qmax_done"], FIRST + z.at(KT, r + 1))
                    if r >= 4:
                        dve.wait_ge(S["tr_done"], FIRST + z.unit(("q", r - 4)) + 1)
                    V.tensor_tensor(heads(qs[r % 4][:, :]), heads(p_q[:, :]), spread(qmax[:, :], DH), ALU.subtract)\
                        .then_inc(S["qsub"], 1)

                def q_total(r):
                    dve.wait_ge(S["qexp"], FIRST + z.at(KT, r + 1))
                    dve.wait_ge(S["qrec_done"], FIRST + z.at(KT, r))
                    V.tensor_reduce(qsum[:, :], heads(qs[r % 4][:, :]), AX.X, ALU.add).then_inc(S["qsum_done"], 1)
                    dve.wait_ge(S["qsum_done"], FIRST + z.at(KT, r + 1))
                    dve.wait_ge(S["qnorm"], FIRST + z.at(KT, max(r - 1, 0)))
                    V.reciprocal(qrec[r % 2][:, :], qsum[:, :]).then_inc(S["qrec_done"], 1)

                def tiny(k):
                    dve.wait_ge(S["route_step"], FIRST + z.before(13, k))

                if z.ffn:
                    dve.wait_ge(S["ss_done"], FIRST + s)
                    dve.wait_ge(S["ss_pow"], FIRST + s - 1)
                    V.tensor_scalar(ss[:, :], p_g[:, 0:KT], 1e-24, None, ALU.max).then_inc(S["ss_out"], 1)
                for r in range(KT):
                    if z.att:
                        if r % 2 == 0:
                            k_max(r // 2)
                        q_shift(r)
                        if r >= 1:
                            q_total(r - 1)
                    if z.ffn and r == 0:
                        dve.wait_ge(S["spread_done"], FIRST + s)
                        dve.wait_ge(S["x1_done"], FIRST + s - 1)
                        V.scalar_tensor_tensor(out=t_sb[:, :], in0=o_sb[:, :], scalar=sc[:, 0:1], in1=p_y[:, :],
                                               op0=ALU.mult, op1=ALU.mult).then_inc(S["t_done"], 1)
                    if z.ffn and r == 1:
                        dve.wait_ge(S["x1_done"], FIRST + s)
                        norm("1", x1, t_sb, s - 1, None)
                    if z.ffn and r == 2:
                        norm_apply("1", x1, t_sb, s - 1)
                    if z.ffn and r == 5:
                        dve.wait_ge(S["lora_done"], FIRST + s)
                        tiny(0)
                        V.tensor_reduce(sm[:, 0:1], p_g[:, ER:ER + NE], AX.X, ALU.max, negate=True)\
                            .then_inc(S["route_max"], 1)
                        dve.wait_ge(S["route_exp"], FIRST + s)
                        V.tensor_reduce(sm[:, 1:2], ex[:, :], AX.X, ALU.max).then_inc(S["route_step"], 1)
                        tiny(1)
                        V.scalar_tensor_tensor(out=tmp[:, :], in0=ex[:, :], scalar=sm[:, 1:2], in1=prio_sb[:, :],
                                               op0=ALU.is_equal, op1=ALU.mult).then_inc(S["route_step"], 1)
                        tiny(2)
                        V.tensor_reduce(sm[:, 2:3], tmp[:, :], AX.X, ALU.max).then_inc(S["route_step"], 1)
                        tiny(3)
                        V.tensor_scalar(sel[:, :], prio_sb[:, :], sm[:, 2:3], None, ALU.is_equal)\
                            .then_inc(S["route_step"], 1)
                        tiny(4)
                        V.scalar_tensor_tensor(out=rt[:, :], in0=sel[:, :], scalar=-4.0, in1=ex[:, :],
                                               op0=ALU.mult, op1=ALU.add).then_inc(S["route_step"], 1)
                        tiny(5)
                        V.tensor_reduce(sm[:, 3:4], rt[:, :], AX.X, ALU.max).then_inc(S["route_step"], 1)
                        tiny(6)
                        V.scalar_tensor_tensor(out=tmp[:, :], in0=rt[:, :], scalar=sm[:, 3:4], in1=prio_sb[:, :],
                                               op0=ALU.is_equal, op1=ALU.mult).then_inc(S["route_step"], 1)
                        tiny(7)
                        V.tensor_reduce(sm[:, 4:5], tmp[:, :], AX.X, ALU.max).then_inc(S["route_step"], 1)
                        tiny(8)
                        V.scalar_tensor_tensor(out=sel[:, :], in0=prio_sb[:, :], scalar=sm[:, 4:5], in1=sel[:, :],
                                               op0=ALU.is_equal, op1=ALU.add).then_inc(S["route_step"], 1)
                        V.tensor_tensor(sm[:, 5:6], sm[:, 1:2], sm[:, 3:4], ALU.add).then_inc(S["route_step"], 1)
                        tiny(10)
                        V.reciprocal(sm[:, 6:7], sm[:, 5:6]).then_inc(S["route_step"], 1)
                        V.tensor_tensor(rt[:, :], ex[:, :], sel[:, :], ALU.mult).then_inc(S["route_step"], 1)
                        tiny(12)
                        V.tensor_scalar(rt[:, :], rt[:, :], sm[:, 6:7], 2.0, ALU.mult, ALU.mult)\
                            .then_inc(S["route_step"], 1)
                        tiny(13)
                        dve.wait_ge(S["h_turned"], FIRST + s - 1)
                        V.tensor_tensor(h_sb[:, :].rearrange("p (e r) -> p e r", e=NE),
                                        p_g[:, 0:ER].rearrange("p (e r) -> p e r", e=NE), spread(rt[:, :], R),
                                        ALU.mult).then_inc(S["h_done"], 1)
                    if z.ffn and r == 6:
                        dve.wait_ge(S["h_turned"], FIRST + s)
                        dve.wait_ge(S["y_done"], FIRST + s - 1)
                        V.tensor_copy(hT[:, :], p_g[:, 2 * P:3 * P]).then_inc(S["hT_out"], 1)
                if z.att:
                    q_total(KT - 1)
                    dve.wait_ge(S["w2_out"], FIRST + s)
                    dve.wait_ge(S["kexp"], FIRST + z.at(MT, MT))
                    V.reciprocal(krec[:, :], ksum[:, :]).then_inc(S["krec_done"], 1)
                if z.ffn:
                    dve.wait_ge(S["y_done"], FIRST + s)
                    dve.wait_ge(S["x1b_done"], FIRST + s)
                    dve.wait_ge(S["x2_free"], FIRST + s - 1)
                    V.scalar_tensor_tensor(out=x2[:, :], in0=p_y[:, :], scalar=tgf[:, 0:1], in1=x1b[:, :],
                                           op0=ALU.mult, op1=ALU.add).then_inc(S["x2_done"], 1)
                    dve.wait_ge(S["x2_done"], FIRST + s)
                    norm("2", x2, t_sb, s - 1, None)
                    norm_apply("2", x2, t_sb, s - 1)
                if z.att:
                    if z.c != BATCH - 1:
                        prepare(s + 1, 1 - z.par, z.half + (1 if z.par else 0))
                        prepare_apply(s + 1, 1 - z.par, s)
                    dve.wait_ge(S["krec_done"], FIRST + s + 1)
                    dve.wait_ge(S["w2_done"], FIRST + s + 1)
                    V.scalar_tensor_tensor(out=w2[:, :, :], in0=p_g[:, :].rearrange("p (m o) -> p m o", m=MT),
                                           scalar=DH ** -0.5, in1=spread(krec[:, :], P), op0=ALU.mult, op1=ALU.mult)\
                        .then_inc(S["w2_out"], 1)

            steps(dve, body)

        @block.tensor
        def _(pe):
            for name in ("avo_done", "tr_done", "k_proj", "q_proj", "k_used", "ss_done", "spread_done", "lora_done",
                         "h_turned", "y_done", "w2_done", "out_done"):
                pe.sem_inc(S[name], 1)
            M, T = nc.tensor.matmul, nc.tensor.transpose

            pe.wait_ge(S["const_pool"], FIRST + 5)
            pe.wait_ge(S["const_in"], 16 * 11)
            for h in range(H):
                mm = M(p_k[:, h * P:(h + 1) * P], ke[0:DH, 0, h * P:(h + 1) * P], ke[0:DH, 1, h * P:(h + 1) * P],
                       start=True, stop=True)
            mm.then_inc(S["avo_done"], 1)
            pe.wait_ge(S["const_act"], FIRST + 3)

            def body(z):
                s = z.s

                def turn(name):
                    kind, r = name
                    i = z.units.index(name)
                    u = z.unit(name)
                    if not (z.fresh and i < 2):
                        pe.wait_ge(S["tr_out"], FIRST + u - 1)
                    for m in range(4):
                        k = 4 * r + m
                        src = {"ctx": lambda: c_sb[z.par][:, k * P:(k + 1) * P],
                               "q": lambda: qs[r % 4][:, m * P:(m + 1) * P],
                               "k": lambda: ke[:, m, r * P:(r + 1) * P],
                               "x": lambda: t_sb[:, k * P:(k + 1) * P],
                               "n": lambda: t_sb[:, k * P:(k + 1) * P]}[kind]()
                        mm = T(p_tr[i % 2][:, m * P:(m + 1) * P], src, ident[:, :])
                    mm.then_inc(S["tr_done"], 1)

                def k_project(m):
                    if m == 0:
                        pe.wait_ge(S["in_lo"], FIRST + z.at(2, 1))
                        pe.wait_ge(S["o_out"], FIRST + s)
                    else:
                        pe.wait_ge(S["kexp"], FIRST + z.at(MT, m))
                    for h in range(2):
                        for n, (a, b) in enumerate(SPLIT):
                            mm = M(p_k[:, h * BANK:(h + 1) * BANK], wk[a][:, m * P:(m + 1) * P],
                                   cc[b][:, h * BANK:(h + 1) * BANK], start=(n == 0), stop=(n == 2))
                    mm.then_inc(S["k_proj"], 1)

                def q_project(r):
                    if r == 0:
                        pe.wait_ge(S["in_lo"], FIRST + z.at(2, 2))
                    pe.wait_ge(S["qsub"], FIRST + z.at(KT, r))
                    for n, (a, b) in enumerate(SPLIT):
                        mm = M(p_q[:, :], xn[a][:, r * P:(r + 1) * P], wq[b][:, :], start=(n == 0), stop=(n == 2))
                    mm.then_inc(S["q_proj"], 1)

                def base(ks):
                    for k in ks:
                        for h in range(2):
                            for n, (a, b) in enumerate(SPLIT):
                                M(p_y[:, h * BANK:(h + 1) * BANK], xT[a][:, k, :], wb[b][:, k, h * BANK:(h + 1) * BANK],
                                  start=(k == 0 and n == 0), stop=False)

                def gather(r):
                    pe.wait_ge(S["tr_out"], FIRST + z.unit(("k", r)) + 1)
                    M(p_g[:, :], cT[:, r, :], keT[r % 2][:, :], start=(r == 0), stop=(r == KT - 1))\
                        .then_inc(S["k_used"], 1)

                if z.ffn:
                    pe.wait_ge(S["sq_done"], FIRST + s)
                    pe.wait_ge(S["w2_out"], FIRST + s)
                    for r in range(KT):
                        mm = M(p_g[:, r:r + 1], sq[:, r * P:(r + 1) * P], ones[:, 0:1], start=True, stop=True)
                    mm.then_inc(S["ss_done"], 1)
                if z.att:
                    pe.wait_ge(c_land[z.par], 16 * z.half + 16)
                    turn(("ctx", 0))
                    turn(("ctx", 1))
                for r in range(KT):
                    if z.att:
                        if r % 2 == 0:
                            k_project(r // 2)
                        q_project(r)
                    if z.ffn and r == 0:
                        pe.wait_ge(S["diag_done"], FIRST + s)
                        pe.wait_ge(S["x2_done"], FIRST + s - 1)
                        for h in range(2):
                            mm = M(p_y[:, h * BANK:(h + 1) * BANK], ones[:, :], diag[:, 4 * h:4 * h + 4, :],
                                   start=True, stop=True)
                        mm.then_inc(S["spread_done"], 1)
                    if z.att and r >= 2:
                        pe.wait_ge(S["qnorm"], FIRST + z.at(KT, r - 1))
                        turn(("q", r - 2))
                    if z.ffn and r == 4:
                        pe.wait_ge(LN["1"]["done"], FIRST + s)
                        turn(("x", 0))
                        turn(("x", 1))
                    if z.ffn and r == 5:
                        pe.wait_ge(S["tr_out"], FIRST + z.unit(("x", 1)) + 1)
                        pe.wait_ge(S["ss_out"], FIRST + s)
                        for k in range(KT):
                            mm = M(p_g[:, 0:ER + NE], xT_f[:, k, :], ar[:, k, :], start=(k == 0), stop=(k == KT - 1))
                        mm.then_inc(S["lora_done"], 1)
                        pe.wait_ge(S["t_done"], FIRST + s)
                        pe.wait_ge(S["xT_lo"], FIRST + s)
                        base(range(0, 2))
                    if z.ffn and r == 6:
                        base(range(2, 4))
                        pe.wait_ge(S["h_done"], FIRST + s)
                        T(p_g[:, 2 * P:3 * P], h_sb[:, :], ident[:, :]).then_inc(S["h_turned"], 1)
                    if z.ffn and r == 7:
                        base(range(4, 6))
                if z.att:
                    pe.wait_ge(S["qnorm"], FIRST + z.at(KT, KT - 1))
                    turn(("q", KT - 2))
                if z.ffn:
                    base(range(6, 8))
                    pe.wait_ge(S["hT_out"], FIRST + s)
                    for h in range(2):
                        mm = M(p_y[:, h * BANK:(h + 1) * BANK], hT[:, :], bm[:, h * BANK:(h + 1) * BANK],
                               start=False, stop=True)
                    mm.then_inc(S["y_done"], 1)
                if z.att:
                    pe.wait_ge(S["qnorm"], FIRST + z.at(KT, KT))
                    turn(("q", KT - 1))
                    pe.wait_ge(S["kexp"], FIRST + z.at(MT, MT))
                    turn(("k", 0))
                    for r in range(1, 6):
                        turn(("k", r))
                        gather(r - 1)
                if z.ffn:
                    pe.wait_ge(LN["2"]["done"], FIRST + s)
                    turn(("n", 0))
                    turn(("n", 1))
                if z.att:
                    for r in range(6, KT):
                        turn(("k", r))
                        gather(r - 1)
                    gather(KT - 1)
                    pe.wait_ge(S["g_out"], FIRST + s + 1)
                    for h in range(H):
                        half = slice(DH * (h % 2), DH * (h % 2) + DH)
                        mm = M(p_g[half, (h // 2) * P:(h // 2 + 1) * P], g_sb[:, h * DH:(h + 1) * DH], avo[:, h, :],
                               start=True, stop=True)
                    mm.then_inc(S["w2_done"], 1)
                    pe.wait_ge(S["w2_out"], FIRST + s + 1)
                    pe.wait_ge(S["tr_out"], FIRST + z.unit(("q", KT - 1)) + 1)
                    for h in range(2):
                        for m in range(MT):
                            mm = M(p_k[:, h * BANK:(h + 1) * BANK], w2[:, m, :], qT[:, m, h * BANK:(h + 1) * BANK],
                                   start=(m == 0), stop=(m == MT - 1))
                    mm.then_inc(S["out_done"], 1)

            steps(pe, body)


def gqa_stage(nc, x_in, xnT, ctxT, mask, gate, Wq, Wk, Wv, Wo, cos_t, sin_t, x_out):
    HD, NH, NKV = 128, 32, 8
    G = NH // NKV
    NB = BANK // SEQ
    NGRP = BATCH // NB
    CAP = 30.0
    SCALE = 0.08838834764831845 / CAP
    NR = 1 + G
    NU = NB * (DM // BANK)
    HALVES = 2

    with ExitStack() as ctx:
        def sb(name, shape, dt=F32):
            return ctx.enter_context(nc.sbuf_tensor("g_" + name, shape, dt))

        def ps(name):
            return ctx.enter_context(nc.psum_tensor("gp_" + name, [P, BANK], F32))

        def sem(name):
            return ctx.enter_context(nc.semaphore("g_" + name))

        operands = {"xn": [P, KT, BANK], "cx": [P, KT, BANK], "wq": [P, KT, G * HD],
                    "wkv": [P, KT, HD],
                    "wo": [P, G, DM],
                    "q": [P, G, BANK],
                    "k": [P, BANK],
                    "v": [P, BANK],
                    "prob0": [P, BANK], "prob1": [P, BANK],
                    "at": [P, G, BANK]}
        with ExitStack() as given_back:
            parts = {n: {"raw": given_back.enter_context(nc.sbuf_tensor(f"g_{n}_raw", shape, F32))}
                     for n, shape in operands.items()}
        for n, shape in operands.items():
            parts[n]["lo"] = sb(n + "_lo", shape, F32R)
        for n, shape in operands.items():
            parts[n]["hi"] = sb(n + "_hi", shape, F32R)
        xn, cx, wq, wkv, wo, q, k, v, at = (parts[n] for n in ("xn", "cx", "wq", "wkv", "wo", "q", "k", "v", "at"))
        prob = [parts["prob0"], parts["prob1"]]
        res = sb("res", [P, NB, DM])
        rot_b = sb("rot_b", [P, BANK])
        rsum = rot_b
        vT = prob[0]["raw"]
        cos_k, sin_k = sb("cos_k", [P, SEQ]), sb("sin_k", [P, SEQ])
        cos_q, sin_q = sb("cos_q", [P, SEQ]), sb("sin_q", [P, SEQ])
        m8 = sb("m8", [P, SEQ // 4], U32)
        mf = rot_b[:, 0:SEQ]
        empty = rot_b[:, SEQ:2 * SEQ]
        sees = rot_b[:, 2 * SEQ:3 * SEQ]
        keep = sb("keep", [P, SEQ])
        ident, ones = sb("ident", [P, P]), sb("ones", [P, P])
        ones_r = sb("ones_r", [P, P], F32R)
        tg = sb("tg", [P, 1])

        p_proj = [ps("p0"), ps("p1")]
        p_s = [ps("s0"), ps("s1")]
        p_pv, p_sum = ps("pv"), ps("sum")
        p_y = [ps("y0"), ps("y1")]

        const_in, const_pool, const_dve = sem("const_in"), sem("const_pool"), sem("const_dve")
        const_pe, const_act = sem("const_pe"), sem("const_act")
        land = {n: [sem(f"{n}_land{i}") for i in range(HALVES)] for n in ("xn", "cx", "wq", "wo")}
        wkv_land = sem("wkv_land")
        xn_hi, cx_hi, wq_hi, wkv_hi, wo_hi = (sem(n + "_hi") for n in ("xn", "cx", "wq", "wkv", "wo"))
        wkv_lo, wo_lo, cx_lo, xn_lo = sem("wkv_lo"), sem("wo_lo"), sem("cx_lo"), sem("xn_lo")
        wq_lo = [sem(f"wq_lo{i}") for i in range(HALVES)]
        res_in, res_out = sem("res_in"), sem("res_out")
        qk_proj, v_proj, vT_out, v_turned = sem("qk_proj"), sem("v_proj"), sem("vT_out"), sem("v_turned")
        v_hi, v_lo = sem("v_hi"), sem("v_lo")
        rot_mul, rot_done, rot_hi, rot_lo = sem("rot_mul"), sem("rot_done"), sem("rot_hi"), sem("rot_lo")
        s_done, tanh_done, exp_done, masked = sem("s_done"), sem("tanh_done"), sem("exp_done"), sem("masked")
        prob_hi, prob_lo = sem("prob_hi"), sem("prob_lo")
        sum_done, pv_done, rsum_done, attn_done = (sem(n) for n in ("sum_done", "pv_done", "rsum_done", "attn_done"))
        at_hi, at_lo, y_done, y_added = sem("at_hi"), sem("at_lo"), sem("y_done"), sem("y_added")

        Wq_v = Wq.rearrange("(k p) (j n) -> j p k n", p=P, j=NKV)
        Wk_v = Wk.rearrange("(k p) (j n) -> j p k n", p=P, j=NKV)
        Wv_v = Wv.rearrange("(k p) (j n) -> j p k n", p=P, j=NKV)
        Wo_v = Wo.rearrange("(j g p) n -> j p g n", p=P, j=NKV)
        res_src = x_in.rearrange("(g b) t d -> g t b d", b=NB)
        res_dst = x_out.rearrange("(g b) t d -> g t b d", b=NB)

        class Step:

            def __init__(self, g, j, first=False, group_start=False, group_end=False, last=False):
                self.g, self.j, self.n = g, j, g * NKV + j
                self.first, self.last = first, last
                self.group_start = group_start and not first
                self.group_end = group_end and not last
                self.j_next = 0 if group_end else j + 1
                self.res_group = g - 1 if self.group_start else g

        def steps(engine, body):
            def group(g, first=False, last=False):
                body(Step(g, 0, first=first, group_start=True))
                with engine.Fori(1, NKV - 1) as j:
                    body(Step(g, j))
                body(Step(g, NKV - 1, group_end=True, last=last))

            group(0, first=True)
            with engine.Fori(1, NGRP - 1) as g:
                group(g)
            group(NGRP - 1, last=True)

        block = ctx.enter_context(nc.Block())

        def one(view, i):
            return view[bass.ds(i, 1)].rearrange("o p k n -> (o p) k n")

        def half(name, i):
            if name in ("xn", "cx"):
                return lambda t: t[:, :, i * (BANK // 2):(i + 1) * (BANK // 2)]
            n = (KT if name == "wq" else G) // 2
            return lambda t: t[:, i * n:(i + 1) * n, :]

        def part(name, i, piece):
            if name in ("xn", "cx"):
                c = (2 * i + piece) * SEQ
                return lambda t: t[:, :, c:c + SEQ]
            n = (KT if name == "wq" else G) // 4
            m = (2 * i + piece) * n
            return lambda t: t[:, m:m + n, :]

        def bcols(b):
            return slice(b * SEQ, (b + 1) * SEQ)

        def heads(t):
            return t.rearrange("p (h t) -> p h t", h=G)

        @block.sync
        def _(sp):
            def load_halves(name, buf, src):
                for i in range(HALVES):
                    sp.dma_start(half(name, i)(buf["raw"]), half(name, i)(src)).then_inc(land[name][i], 16)

            def load_acts(name, buf, src, g):
                for b in range(NB):
                    sp.dma_start(buf["raw"][:, :, bcols(b)], one(src, g * NB + b))\
                        .then_inc(land[name][b // 2], 16)

            def load_wkv(src, j):
                sp.dma_start(wkv["raw"][:, :, :], one(src, j)).then_inc(wkv_land, 16)

            for dst, src in ((cos_k, cos_t), (sin_k, sin_t), (m8, mask), (tg, gate)):
                sp.dma_start(dst[:, :], src).then_inc(const_in, 16)
            load_wkv(Wk_v, 0)
            load_acts("cx", cx, ctxT, 0)
            load_halves("wq", wq, one(Wq_v, 0))
            load_acts("xn", xn, xnT, 0)
            sp.dma_start(res[:, :, :], one(res_src, 0)).then_inc(res_in, 16)
            sp.wait_ge(qk_proj, FIRST + 1)
            load_wkv(Wv_v, 0)

            def body(z):
                n = z.n
                if not z.last:
                    sp.wait_ge(qk_proj, FIRST + n * NR + NR)
                    if z.group_end:
                        load_acts("xn", xn, xnT, z.g + 1)
                    else:
                        load_halves("wq", wq, one(Wq_v, z.j_next))
                    sp.wait_ge(v_proj, FIRST + n + 1)
                    load_wkv(Wk_v, z.j_next)
                    if z.group_end:
                        load_acts("cx", cx, ctxT, z.g + 1)
                        load_halves("wq", wq, one(Wq_v, z.j_next))
                sp.wait_ge(y_done, FIRST + n * NU)
                load_halves("wo", wo, one(Wo_v, z.j))
                if z.group_start:
                    sp.wait_ge(y_added, FIRST + n * NU)
                    sp.dma_start(one(res_dst, z.g - 1), res[:, :, :]).then_inc(res_out, 16)
                if not z.last:
                    sp.wait_ge(qk_proj, FIRST + (n + 1) * NR + 1)
                    load_wkv(Wv_v, z.j_next)
                if z.group_start:
                    sp.wait_ge(res_out, z.g * 16)
                    sp.dma_start(res[:, :, :], one(res_src, z.g)).then_inc(res_in, 16)

            steps(sp, body)
            sp.wait_ge(y_added, FIRST + NGRP * NKV * NU)
            sp.dma_start(one(res_dst, NGRP - 1), res[:, :, :]).then_inc(res_out, 16)
            sp.wait_ge(res_out, 16 * NGRP)

        def subtract_hi(engine, buf, view):
            return engine.tensor_tensor(view(buf["lo"]), view(buf["raw"]), view(buf["hi"]).bitcast(F32), ALU.subtract)

        @block.gpsimd
        def _(pool):
            for done in (const_pool, xn_lo, wo_lo, rot_done, rot_lo, prob_lo, at_lo, wq_lo[0]):
                pool.sem_inc(done, 1)
            nc.gpsimd.memset(ones[:, :], 1.0).then_inc(const_pool, 1)
            nc.gpsimd.memset(ident[:, :], 0.0).then_inc(const_pool, 1)
            pool.wait_ge(const_pool, FIRST + 2)
            nc.gpsimd.affine_select(out=ident[:, :], in_=ident[:, :], compare_op=ALU.not_equal, fill=1.0,
                                    base=0, pattern=[[-1, P]], channel_multiplier=1).then_inc(const_pool, 1)

            def xn_split(g):
                for i in range(HALVES):
                    for m in range(2):
                        pool.wait_ge(xn_hi, FIRST + g * 4 + 2 * i + m + 1)
                        subtract_hi(nc.gpsimd, xn, part("xn", i, m)).then_inc(xn_lo, 1)

            def wq_split(n):
                for m in range(2):
                    pool.wait_ge(wq_hi, FIRST + n * 4 + m + 1)
                    subtract_hi(nc.gpsimd, wq, part("wq", 0, m)).then_inc(wq_lo[0], 1)

            def wo_split(n, m):
                pool.wait_ge(wo_hi, FIRST + n * 4 + m + 1)
                subtract_hi(nc.gpsimd, wo, part("wo", m // 2, m % 2)).then_inc(wo_lo, 1)

            def rotated(n, i):
                buf, view = (k, lambda t: t[:, :]) if i == 0 else (q, lambda t: t[:, i - 1, :])
                pool.wait_ge(rot_mul, FIRST + n * NR + i + 1)
                dst = view(buf["raw"])
                nc.gpsimd.tensor_tensor(dst, dst, rot_b[:, :], ALU.add).then_inc(rot_done, 1)
                pool.wait_ge(rot_hi, FIRST + n * NR + i + 1)
                subtract_hi(nc.gpsimd, buf, view).then_inc(rot_lo, 1)

            xn_split(0)
            wq_split(0)
            for i in range(NR):
                rotated(0, i)

            def body(z):
                n = z.n

                def prob_split(b):
                    pool.wait_ge(prob_hi, FIRST + n * NB + b + 1)
                    subtract_hi(nc.gpsimd, prob[b % 2], lambda t: t[:, :]).then_inc(prob_lo, 1)

                def attn_split(b):
                    pool.wait_ge(at_hi, FIRST + n * NB + b + 1)
                    subtract_hi(nc.gpsimd, at, lambda t: t[:, :, bcols(b)]).then_inc(at_lo, 1)

                prob_split(0)
                prob_split(1)
                attn_split(0)
                prob_split(2)
                if z.group_end:
                    xn_split(z.g + 1)
                attn_split(1)
                prob_split(3)
                attn_split(2)
                if not z.last:
                    wq_split(n + 1)
                attn_split(3)
                for i in range(NR):
                    if not z.last:
                        rotated(n + 1, i)
                    if i < 4:
                        wo_split(n, i)

            steps(pool, body)

        @block.scalar
        def _(act):
            for done in (const_act, xn_hi, cx_hi, wq_hi, wo_hi, wkv_hi, rot_hi, vT_out, tanh_done, exp_done, prob_hi,
                         at_hi, v_hi):
                act.sem_inc(done, 1)
            A = nc.scalar.activation
            act.wait_ge(const_in, 64)
            A(tg[:, :], tg[:, :], ACT.Tanh).then_inc(const_act, 1)
            act.wait_ge(const_pool, FIRST + 1)
            A(ones_r[:, :], ones[:, :], ACT.Copy).then_inc(const_act, 1)

            def round_hi(buf, view):
                return A(view(buf["hi"]), view(buf["raw"]), ACT.Copy)

            def quarters(name, buf, count, done, which):
                for m in which:
                    loads = 2 if name in ("xn", "cx") else 1
                    act.wait_ge(land[name][m // 2], 16 * loads * count)
                    round_hi(buf, part(name, m // 2, m % 2)).then_inc(done, 1)

            def wkv_round(count):
                act.wait_ge(wkv_land, 16 * count)
                round_hi(wkv, lambda t: t[:, :, :]).then_inc(wkv_hi, 1)

            def rot_round(n, i):
                buf, view = (k, lambda t: t[:, :]) if i == 0 else (q, lambda t: t[:, i - 1, :])
                act.wait_ge(rot_done, FIRST + n * NR + i + 1)
                round_hi(buf, view).then_inc(rot_hi, 1)

            def value_out(n):
                act.wait_ge(v_proj, FIRST + n + 1)
                A(vT[:, :], p_proj[1][:, :], ACT.Copy).then_inc(vT_out, 1)

            wkv_round(1)
            quarters("cx", cx, 1, cx_hi, range(4))
            quarters("wq", wq, 1, wq_hi, range(4))
            quarters("xn", xn, 1, xn_hi, range(4))
            rot_round(0, 0)
            wkv_round(2)
            for i in range(1, NR):
                rot_round(0, i)
            value_out(0)

            def body(z):
                n = z.n

                def softmax(b):
                    e = prob[b % 2]["raw"][:, :]
                    act.wait_ge(s_done, FIRST + n * NB + b + 1)
                    act.wait_ge(pv_done, FIRST + n * NB + max(b - 1, 0))
                    if b == 0:
                        act.wait_ge(v_turned, FIRST + n + 1)
                    A(e, p_s[b % 2][:, :], ACT.Tanh, scale=SCALE).then_inc(tanh_done, 1)
                    act.wait_ge(tanh_done, FIRST + n * NB + b + 1)
                    A(e, e, ACT.Exp, scale=CAP).then_inc(exp_done, 1)

                def softmax_hi(b):
                    act.wait_ge(masked, FIRST + n * NB + b + 1)
                    round_hi(prob[b % 2], lambda t: t[:, :]).then_inc(prob_hi, 1)

                def attn_hi(b):
                    act.wait_ge(attn_done, FIRST + n * NB + b + 1)
                    round_hi(at, lambda t: t[:, :, bcols(b)]).then_inc(at_hi, 1)

                act.wait_ge(v_turned, FIRST + n + 1)
                act.wait_ge(pv_done, FIRST + n * NB)
                A(v["raw"][:, :], p_pv[:, :], ACT.Copy).then_inc(v_hi, 1)
                softmax(0)
                act.wait_ge(v_hi, FIRST + 2 * n + 1)
                round_hi(v, lambda t: t[:, :]).then_inc(v_hi, 1)
                softmax_hi(0)
                softmax(1)
                softmax_hi(1)
                if not z.last:
                    wkv_round(2 * n + 3)
                    if z.group_end:
                        quarters("xn", xn, z.g + 2, xn_hi, range(4))
                attn_hi(0)
                softmax(2)
                softmax_hi(2)
                attn_hi(1)
                if z.group_end:
                    quarters("cx", cx, z.g + 2, cx_hi, range(4))
                softmax(3)
                softmax_hi(3)
                attn_hi(2)
                if not z.last:
                    quarters("wq", wq, n + 2, wq_hi, range(4))
                attn_hi(3)
                for i in range(NR):
                    if not z.last:
                        rot_round(n + 1, i)
                        if i == 1:
                            wkv_round(2 * n + 4)
                    if i < 4:
                        quarters("wo", wo, n + 1, wo_hi, (i,))
                if not z.last:
                    value_out(n + 1)

            steps(act, body)

        @block.vector
        def _(dve):
            for done in (const_dve, cx_lo, wkv_lo, rot_mul, y_added, masked, rsum_done, attn_done, v_lo,
                         wq_lo[1]):
                dve.sem_inc(done, 1)
            V = nc.vector
            dve.wait_ge(const_in, 64)
            V.tensor_copy(mf, m8[:, :].bitcast(U8)).then_inc(const_dve, 1)
            dve.wait_ge(const_pe, FIRST + 1)
            V.tensor_copy(keep[:, :], p_s[0][:, 0:SEQ]).then_inc(const_dve, 1)
            dve.wait_ge(const_pe, FIRST + 2)
            V.tensor_scalar(empty, p_s[0][:, 0:SEQ], 0.5, None, ALU.is_lt).then_inc(const_dve, 1)
            V.tensor_scalar(sees, p_s[0][:, 0:SEQ], 0.5, None, ALU.is_ge).then_inc(const_dve, 1)
            dve.wait_ge(const_dve, FIRST + 4)
            V.tensor_tensor(keep[:, :], keep[:, :], empty, ALU.add).then_inc(const_dve, 1)
            V.tensor_tensor(cos_q[:, :], cos_k[:, :], sees, ALU.mult).then_inc(const_dve, 1)
            V.tensor_tensor(sin_q[:, :], sin_k[:, :], sees, ALU.mult).then_inc(const_dve, 1)
            dve.wait_ge(const_act, FIRST + 1)
            dve.wait_ge(const_dve, FIRST + 7)

            def cx_split(g):
                for m in range(4):
                    dve.wait_ge(cx_hi, FIRST + g * 4 + m + 1)
                    subtract_hi(V, cx, part("cx", m // 2, m % 2)).then_inc(cx_lo, 1)

            def wkv_split(count):
                dve.wait_ge(wkv_hi, FIRST + count)
                subtract_hi(V, wkv, lambda t: t[:, :, :]).then_inc(wkv_lo, 1)

            def wq_split(n):
                for m in range(2):
                    dve.wait_ge(wq_hi, FIRST + n * 4 + m + 3)
                    subtract_hi(V, wq, part("wq", 1, m)).then_inc(wq_lo[1], 1)

            def rotate(n, i):
                src = p_proj[i % 2]
                a = k["raw"][:, :] if i == 0 else q["raw"][:, i - 1, :]
                cos, sin = (cos_k, sin_k) if i == 0 else (cos_q, sin_q)
                mid = P // 2
                dve.wait_ge(qk_proj, FIRST + n * NR + i + 1)
                dve.wait_ge(rot_done, FIRST + n * NR + i)
                if i == 0:
                    dve.wait_ge(s_done, FIRST + n * NB)

                def w(t, lo_, hi_):
                    return t[lo_:hi_, :].rearrange("p (o t) -> p o t", o=1).to_broadcast([hi_ - lo_, NB, SEQ])

                def by_batch(t):
                    return t.rearrange("p (b t) -> p b t", b=NB)

                V.tensor_tensor(by_batch(a), by_batch(src[:, :]), w(cos, 0, P), ALU.mult)
                V.tensor_tensor(by_batch(rot_b[mid:P, :]), by_batch(src[0:mid, :]), w(sin, 0, mid), ALU.mult)
                V.tensor_tensor(by_batch(rot_b[0:mid, :]), by_batch(src[mid:P, :]), w(sin, mid, P), ALU.mult)\
                    .then_inc(rot_mul, 1)

            cx_split(0)
            wkv_split(1)
            wq_split(0)
            rotate(0, 0)
            wkv_split(2)
            for i in range(1, NR):
                rotate(0, i)

            def add_output(n_out, u):
                b, h = u // 2, u % 2
                r = res[:, b, h * BANK:(h + 1) * BANK]
                dve.wait_ge(y_done, FIRST + n_out * NU + u + 1)
                if u == 0:
                    dve.wait_ge(y_added, FIRST + n_out * NU)
                V.scalar_tensor_tensor(out=r, in0=p_y[u % 2][:, :], scalar=tg[:, 0:1], in1=r,
                                       op0=ALU.mult, op1=ALU.add).then_inc(y_added, 1)

            def body(z):
                n = z.n

                def add(*units):
                    if not z.first:
                        for u in units:
                            add_output(n - 1, u)

                def mask_probs(b):
                    e = prob[b % 2]["raw"][:, :]
                    dve.wait_ge(exp_done, FIRST + n * NB + b + 1)
                    V.tensor_tensor(heads(e), heads(e), keep[:, :].rearrange("p (o t) -> p o t", o=1)
                                    .to_broadcast([P, G, SEQ]), ALU.mult).then_inc(masked, 1)

                def normalise(b):
                    dve.wait_ge(sum_done, FIRST + n * NB + b + 1)
                    if b == 0:
                        dve.wait_ge(rot_done, FIRST + (n + 1) * NR)
                    dve.wait_ge(attn_done, FIRST + n * NB + b)
                    V.reciprocal(rsum[:, :], p_sum[:, :]).then_inc(rsum_done, 1)
                    dve.wait_ge(rsum_done, FIRST + n * NB + b + 1)
                    dve.wait_ge(pv_done, FIRST + n * NB + b + 1)
                    V.tensor_tensor(at["raw"][:, :, bcols(b)], heads(p_pv[:, :]), heads(rsum[:, :]), ALU.mult)\
                        .then_inc(attn_done, 1)

                if not z.first:
                    dve.wait_ge(res_in, 16 * z.res_group + 16)
                add(0)
                mask_probs(0)
                dve.wait_ge(v_hi, FIRST + 2 * n + 2)
                subtract_hi(V, v, lambda t: t[:, :]).then_inc(v_lo, 1)
                add(1)
                mask_probs(1)
                normalise(0)
                add(2)
                mask_probs(2)
                add(3)
                if not z.last and not z.group_end:
                    wkv_split(2 * n + 3)
                normalise(1)
                add(4)
                if z.group_end:
                    cx_split(z.g + 1)
                    wkv_split(2 * n + 3)
                mask_probs(3)
                add(5)
                normalise(2)
                add(6, 7)
                if not z.last:
                    wq_split(n + 1)
                normalise(3)
                if not z.last:
                    dve.wait_ge(attn_done, FIRST + (n + 1) * NB)
                    for i in range(NR):
                        rotate(n + 1, i)
                        if i == 1:
                            wkv_split(2 * n + 4)

            steps(dve, body)
            for u in range(NU):
                add_output(NGRP * NKV - 1, u)

        @block.tensor
        def _(pe):
            for done in (const_pe, qk_proj, v_proj, v_turned, s_done, sum_done, pv_done, y_done):
                pe.sem_inc(done, 1)
            M, T = nc.tensor.matmul, nc.tensor.transpose
            pe.wait_ge(const_dve, FIRST + 1)
            pe.wait_ge(const_pool, FIRST + 3)
            T(p_s[0][:, 0:P], mf, ident[:, :]).then_inc(const_pe, 1)
            pe.wait_ge(const_dve, FIRST + 2)
            M(p_s[0][:, 0:SEQ], ones[:, :], keep[:, :], start=True, stop=True).then_inc(const_pe, 1)
            pe.wait_ge(const_dve, FIRST + 7)
            pe.wait_ge(const_act, FIRST + 2)

            def projection(bank, w, cols, x):
                for i in range(KT):
                    for t, (a, b) in enumerate(SPLIT):
                        mm = M(bank[:, :], w[a][:, i, cols], x[b][:, i, :],
                               start=(i == 0 and t == 0), stop=(i == KT - 1 and t == 2))
                return mm

            def project(n):
                pe.wait_ge(wkv_lo, FIRST + 2 * n + 1)
                pe.wait_ge(rot_mul, FIRST + n * NR)
                projection(p_proj[0], wkv, slice(0, HD), cx).then_inc(qk_proj, 1)
                pe.wait_ge(vT_out, FIRST + n)
                for i in range(HALVES):
                    pe.wait_ge(wq_lo[i], FIRST + 2 * n + 2)
                for h in range(G):
                    if h >= 1:
                        pe.wait_ge(rot_mul, FIRST + n * NR + h)
                    projection(p_proj[(h + 1) % 2], wq, slice(h * HD, (h + 1) * HD), xn).then_inc(qk_proj, 1)
                pe.wait_ge(wkv_lo, FIRST + 2 * n + 2)
                pe.wait_ge(rot_mul, FIRST + n * NR + G)
                projection(p_proj[1], wkv, slice(0, HD), cx).then_inc(v_proj, 1)

            def turn_value(n):
                pe.wait_ge(vT_out, FIRST + n + 1)
                pe.wait_ge(attn_done, FIRST + n * NB)
                for b in range(NB):
                    mm = T(p_pv[:, bcols(b)], vT[:, bcols(b)], ident[:, :])
                mm.then_inc(v_turned, 1)

            def scores(n, b):
                if b == 0:
                    pe.wait_ge(rot_lo, FIRST + (n + 1) * NR)
                pe.wait_ge(tanh_done, FIRST + n * NB + max(b - 1, 0))
                for t, (p, r) in enumerate(SPLIT):
                    mm = M(heads(p_s[b % 2][:, :]), k[p][:, bcols(b)], q[r][:, :, bcols(b)],
                           start=(t == 0), stop=(t == 2))
                mm.then_inc(s_done, 1)

            def values(n, b):
                pe.wait_ge(prob_lo, FIRST + n * NB + b + 1)
                pe.wait_ge(attn_done, FIRST + n * NB + b)
                if b == 0:
                    pe.wait_ge(v_lo, FIRST + n + 1)
                for t, r in enumerate(("hi", "lo")):
                    mm = M(p_sum[:, :], ones_r[:, :], prob[b % 2][r][:, :], start=(t == 0), stop=(t == 1))
                mm.then_inc(sum_done, 1)
                for t, (p, r) in enumerate(SPLIT):
                    mm = M(p_pv[:, :], v[p][:, bcols(b)], prob[b % 2][r][:, :], start=(t == 0), stop=(t == 2))
                mm.then_inc(pv_done, 1)

            def output(n, u):
                b, half_ = u // 2, u % 2
                if u == 0:
                    pe.wait_ge(wo_lo, FIRST + (n + 1) * 4)
                if half_ == 0:
                    pe.wait_ge(at_lo, FIRST + n * NB + b + 1)
                pe.wait_ge(y_added, FIRST + n * NU + max(u - 1, 0))
                for h in range(G):
                    for t, (p, r) in enumerate(SPLIT):
                        mm = M(p_y[u % 2][:, :], at[p][:, h, bcols(b)], wo[r][:, h, half_ * BANK:(half_ + 1) * BANK],
                               start=(h == 0 and t == 0), stop=(h == G - 1 and t == 2))
                mm.then_inc(y_done, 1)

            def attend(n, first=False):
                def out(*units):
                    if not first:
                        for u in units:
                            output(n - 1, u)

                out(0)
                turn_value(n)
                scores(n, 0)
                scores(n, 1)
                out(1)
                values(n, 0)
                out(2)
                scores(n, 2)
                out(3)
                values(n, 1)
                out(4)
                scores(n, 3)
                out(5)
                values(n, 2)
                out(6, 7)
                values(n, 3)

            last = NGRP * NKV - 1
            project(0)
            attend(0, first=True)
            project(1)
            with pe.Fori(1, last) as n:
                attend(n)
                project(n + 1)
            attend(last)
            for u in range(NU):
                output(last, u)


def sign_ffn_stage(nc, x_in, gate, signW, bias, gate_wT, in_scale, out_scale, x_out):
    NE = 8
    with ExitStack() as ctx:
        def sb(name, shape, dt=F32):
            return ctx.enter_context(nc.sbuf_tensor("f_" + name, shape, dt))

        def ps(name, cols):
            return ctx.enter_context(nc.psum_tensor("fp_" + name, [P, cols], F32))

        def sem(name):
            return ctx.enter_context(nc.semaphore("f_" + name))

        w_raw = [sb(f"w_raw{i}", [P, DM]) for i in range(2)]
        w = sb("w", [P, KT, DM], F32R)
        gw = sb("gw", [P, KT, NE])
        ics = sb("ics", [NE, DM])
        ocs = sb("ocs", [NE, DM])
        tgb = sb("tgb", [P, DM])
        tg = sb("tg", [P, 1])
        ident = sb("ident", [P, P])
        eps = sb("eps", [P, 1])
        half_neg = sb("half_neg", [P, 1])
        x_sb = [sb(f"x{i}", [P, DM]) for i in range(4)]
        stats = sb("stats", [P, 2, 6])
        mv = sb("mv", [P, 2])
        rstd = sb("rstd", [P, 1])
        xn = [sb(f"xn{i}", [P, DM]) for i in range(2)]
        xnT = sb("xnT", [P, DM])
        small = sb("small", [P, 4])
        rt = sb("rt", [P, NE])
        rT = sb("rT", [NE, P])
        xs = sb("xs", [P, DM])
        xs_part = {(h, i): sb(f"xs_{h}{i}", [P, DM], F32R) for h in ("hi", "lo") for i in range(2)}
        osc = [sb(f"osc{i}", [P, DM]) for i in range(2)]
        xb = [sb(f"xb{i}", [P, DM]) for i in range(2)]
        y = sb("y", [P, DM])
        out_sb = [sb(f"out{i}", [P, DM]) for i in range(2)]

        p_t, p_o, p_y, p_l = ps("t", DM), ps("o", DM), ps("y", DM), ps("l", BANK)

        const_in = sem("const_in")
        const_pool = sem("const_pool")
        gate_done = sem("gate_done")
        w_in = [sem(f"w_in{i}") for i in range(2)]
        w_ready = sem("w_ready")
        x_in_s = [sem(f"x_in{i}") for i in range(4)]
        moments = sem("moments")
        rstd_done = sem("rstd_done")
        xn_done = sem("xn_done")
        turned = sem("turned")
        xnT_out = sem("xnT_out")
        logits_done = sem("logits_done")
        route_steps = sem("route_steps")
        exp_done = sem("exp_done")
        rt_turned = sem("rt_turned")
        rT_out = sem("rT_out")
        in_scaled = sem("in_scaled")
        out_scaled = sem("out_scaled")
        xs_done = sem("xs_done")
        xs_hi = sem("xs_hi")
        xs_lo = sem("xs_lo")
        osc_out = sem("osc_out")
        xb_done = sem("xb_done")
        main_done = sem("main_done")
        y_done = sem("y_done")
        out_ready = sem("out_ready")
        out_free = sem("out_free")
        out_store = [sem(f"out_store{i}") for i in range(2)]

        block = ctx.enter_context(nc.Block())

        def batch(view, i):
            return view[bass.ds(i, 1)].rearrange("o p n -> (o p) n")

        QUADS = BATCH // 4

        @block.sync
        def _(sp):
            sp.sem_inc(out_free, 1)
            sp.dma_start(gw[:, :, :], gate_wT.rearrange("(k p) e -> p k e", p=P)).then_inc(const_in, 16)
            sp.dma_start(ics[:, :], in_scale).then_inc(const_in, 16)
            sp.dma_start(ocs[:, :], out_scale).then_inc(const_in, 16)
            sp.dma_start(tgb[:, :], bias).then_inc(const_in, 16)
            sp.dma_start(tg[:, :], gate).then_inc(const_in, 16)
            for i in range(4):
                sp.dma_start(x_sb[i][:, :], x_in[i]).then_inc(x_in_s[i], 16)
            for k in range(KT):
                if k >= 2:
                    sp.wait_ge(w_ready, FIRST + k - 1)
                sp.dma_start(w_raw[k % 2][:, :], signW[k * P:(k + 1) * P, :]).then_inc(w_in[k % 2], 16)

            def step(q, c, more):
                sp.wait_ge(out_ready, FIRST + q * 4 + c + 1)
                sp.dma_start(batch(x_out, q * 4 + c), out_sb[c % 2][:, :]).then_inc(out_store[c % 2], 16)
                sp.wait_ge(out_store[c % 2], (q * 2 + c // 2) * 16 + 16)
                sp.sem_inc(out_free, 1)
                if more:
                    sp.wait_ge(xb_done, FIRST + q * 4 + c + 1)
                    sp.dma_start(x_sb[c][:, :], batch(x_in, q * 4 + c + 4)).then_inc(x_in_s[c], 16)

            with sp.Fori(0, QUADS - 1) as q:
                for c in range(4):
                    step(q, c, True)
            for c in range(4):
                step(QUADS - 1, c, False)
            for i in range(2):
                sp.wait_ge(out_store[i], 16 * BATCH // 2)

        @block.gpsimd
        def _(pool):
            for done in (const_pool, rstd_done, xs_lo, xb_done, out_ready):
                pool.sem_inc(done, 1)
            nc.gpsimd.memset(eps[:, :], EPS).then_inc(const_pool, 1)
            nc.gpsimd.memset(half_neg[:, :], -0.5).then_inc(const_pool, 1)
            nc.gpsimd.memset(ident[:, :], 0.0).then_inc(const_pool, 1)
            pool.wait_ge(const_pool, FIRST + 3)
            nc.gpsimd.affine_select(out=ident[:, :], in_=ident[:, :], compare_op=ALU.not_equal, fill=1.0,
                                    base=0, pattern=[[-1, P]], channel_multiplier=1).then_inc(const_pool, 1)
            pool.wait_ge(gate_done, FIRST + 1)
            pool.wait_ge(const_in, 80)
            nc.gpsimd.tensor_scalar(tgb[:, :], tgb[:, :], tg[:, 0:1], None, ALU.mult).then_inc(const_pool, 1)
            pool.wait_ge(const_pool, FIRST + 5)

            def norm(q, c):
                b = q * 4 + c
                pool.wait_ge(moments, FIRST + 4 * b + 4)
                pool.wait_ge(xn_done, FIRST + b)
                nc.gpsimd.tensor_tensor(rstd[:, :], mv[:, 1:2], eps[:, :], ALU.add).then_inc(rstd_done, 1)
                pool.wait_ge(rstd_done, FIRST + 2 * b + 1)
                nc.gpsimd.tensor_tensor(rstd[:, :], rstd[:, :], half_neg[:, :], ALU.pow).then_inc(rstd_done, 1)

            def scale(q, c):
                b, i = q * 4 + c, c % 2
                pool.wait_ge(xs_hi, FIRST + b + 1)
                nc.gpsimd.tensor_tensor(xs_part["lo", i][:, :], xs[:, :], xs_part["hi", i][:, :].bitcast(F32),
                                        ALU.subtract).then_inc(xs_lo, 1)
                pool.wait_ge(x_in_s[c % 4], 16 * (q + c // 4) + 16)
                pool.wait_ge(out_ready, FIRST + q * 4 + max(c - 1, 0))
                nc.gpsimd.tensor_tensor(xb[i][:, :], x_sb[c % 4][:, :], tgb[:, :], ALU.add).then_inc(xb_done, 1)

            def finish(q, c):
                b, i = q * 4 + c, c % 2
                pool.wait_ge(y_done, FIRST + b + 1)
                pool.wait_ge(xb_done, FIRST + b + 1)
                pool.wait_ge(out_free, FIRST + q * 4 + max(c - 1, 0))
                nc.gpsimd.tensor_tensor(out_sb[i][:, :], y[:, :], xb[i][:, :], ALU.add).then_inc(out_ready, 1)

            norm(0, 0)
            norm(0, 1)
            scale(0, 0)

            def step(q, c, last):
                if not (last and c >= 2):
                    norm(q, c + 2)
                if not (last and c == 3):
                    scale(q, c + 1)
                finish(q, c)

            with pool.Fori(0, QUADS - 1) as q:
                for c in range(4):
                    step(q, c, False)
            for c in range(4):
                step(QUADS - 1, c, True)

        @block.scalar
        def _(act):
            for done in (gate_done, w_ready, xnT_out, exp_done, osc_out, xs_hi):
                act.sem_inc(done, 1)
            act.wait_ge(const_in, 80)
            nc.scalar.activation(tg[:, :], tg[:, :], ACT.Tanh).then_inc(gate_done, 1)
            act.wait_ge(gate_done, FIRST + 1)
            for k in range(KT):
                act.wait_ge(w_in[k % 2], 16 * (k // 2) + 16)
                nc.scalar.activation(w[:, k, :], w_raw[k % 2][:, :], ACT.Sign).then_inc(w_ready, 1)

            def route(q, c):
                b, i = q * 4 + c, c % 2
                act.wait_ge(turned, FIRST + b + 1)
                act.wait_ge(xs_done, FIRST + b)
                nc.scalar.activation(xnT[:, :], p_t[:, :], ACT.Copy).then_inc(xnT_out, 1)
                act.wait_ge(route_steps, FIRST + 3 * b + 1)
                act.wait_ge(rt_turned, FIRST + b)
                nc.scalar.activation(rt[:, :], p_l[:, 0:NE], ACT.Exp, bias=small[:, 0:1],
                                     accum_out=small[:, 1:2]).then_inc(exp_done, 1)
                act.wait_ge(out_scaled, FIRST + b + 1)
                act.wait_ge(y_done, FIRST + q * 4 + max(c - 1, 0))
                nc.scalar.activation(osc[i][:, :], p_o[:, :], ACT.Identity, scale=tg[:, 0:1]).then_inc(osc_out, 1)
                act.wait_ge(xs_done, FIRST + b + 1)
                act.wait_ge(main_done, FIRST + q * 4 + max(c - 1, 0))
                nc.scalar.activation(xs_part["hi", i][:, :], xs[:, :], ACT.Copy).then_inc(xs_hi, 1)

            route(0, 0)

            def step(q, c, last):
                if not (last and c == 3):
                    route(q, c + 1)

            with act.Fori(0, QUADS - 1) as q:
                for c in range(4):
                    step(q, c, False)
            for c in range(4):
                step(QUADS - 1, c, True)

        @block.vector
        def _(dve):
            for done in (moments, xn_done, route_steps, rT_out, xs_done, y_done):
                dve.sem_inc(done, 1)
            def norm(q, c):
                b, i = q * 4 + c, c % 2
                x = x_sb[c % 4]
                dve.wait_ge(x_in_s[c % 4], 16 * (q + c // 4) + 16)
                dve.wait_ge(moments, FIRST + 4 * b)
                for h in range(2):
                    nc.vector.bn_stats(stats[:, h, :], x[:, h * BANK:(h + 1) * BANK]).then_inc(moments, 1)
                dve.wait_ge(moments, FIRST + 4 * b + 2)
                dve.wait_ge(rstd_done, FIRST + 2 * b)
                dve.sem_inc(moments, 1)
                nc.vector.bn_aggr(mv[:, :], stats[:, :, :]).then_inc(moments, 1)
                dve.wait_ge(rstd_done, FIRST + 2 * b + 2)
                dve.wait_ge(turned, FIRST + q * 4 + max(c - 1, 0))
                nc.vector.tensor_scalar(xn[i][:, :], x[:, :], mv[:, 0:1], rstd[:, 0:1], ALU.subtract, ALU.mult)\
                    .then_inc(xn_done, 1)

            def route(q, c):
                b = q * 4 + c
                dve.wait_ge(logits_done, FIRST + b + 1)
                dve.wait_ge(route_steps, FIRST + 3 * b)
                nc.vector.tensor_reduce(small[:, 0:1], p_l[:, 0:NE], AX.X, ALU.max, negate=True)\
                    .then_inc(route_steps, 1)
                dve.wait_ge(exp_done, FIRST + b + 1)
                nc.vector.reciprocal(small[:, 2:3], small[:, 1:2]).then_inc(route_steps, 1)
                dve.wait_ge(route_steps, FIRST + 3 * b + 2)
                nc.vector.tensor_scalar(rt[:, :], rt[:, :], small[:, 2:3], None, ALU.mult).then_inc(route_steps, 1)
                dve.wait_ge(rt_turned, FIRST + b + 1)
                nc.vector.tensor_copy(rT[:, :], p_l[0:NE, P:2 * P]).then_inc(rT_out, 1)

            def scale(q, c):
                b = q * 4 + c
                dve.wait_ge(in_scaled, FIRST + b + 1)
                dve.wait_ge(xs_lo, FIRST + b)
                nc.vector.tensor_tensor(xs[:, :], p_t[:, :], xnT[:, :], ALU.mult).then_inc(xs_done, 1)

            def finish(q, c):
                b, i = q * 4 + c, c % 2
                dve.wait_ge(main_done, FIRST + b + 1)
                dve.wait_ge(osc_out, FIRST + b + 1)
                dve.wait_ge(out_ready, FIRST + b)
                nc.vector.tensor_tensor(y[:, :], p_y[:, :], osc[i][:, :], ALU.mult).then_inc(y_done, 1)

            norm(0, 0)
            norm(0, 1)
            route(0, 0)
            scale(0, 0)

            def step(q, c, last):
                if not (last and c == 3):
                    route(q, c + 1)
                if not (last and c >= 2):
                    norm(q, c + 2)
                if not (last and c == 3):
                    scale(q, c + 1)
                finish(q, c)

            with dve.Fori(0, QUADS - 1) as q:
                for c in range(4):
                    step(q, c, False)
            for c in range(4):
                step(QUADS - 1, c, True)

        @block.tensor
        def _(pe):
            for done in (turned, logits_done, rt_turned, in_scaled, out_scaled, main_done):
                pe.sem_inc(done, 1)
            def turn(q, c):
                b = q * 4 + c
                pe.wait_ge(xn_done, FIRST + b + 1)
                pe.wait_ge(xs_done, FIRST + b)
                for k in range(KT):
                    mm = nc.tensor.transpose(p_t[:, k * P:(k + 1) * P], xn[c % 2][:, k * P:(k + 1) * P], ident[:, :])
                mm.then_inc(turned, 1)

            def logits(q, c):
                b = q * 4 + c
                pe.wait_ge(xnT_out, FIRST + b + 1)
                pe.wait_ge(rT_out, FIRST + b)
                for k in range(KT):
                    mm = nc.tensor.matmul(p_l[:, 0:NE], xnT[:, k * P:(k + 1) * P], gw[:, k, :],
                                          start=(k == 0), stop=(k == KT - 1))
                mm.then_inc(logits_done, 1)

            def turn_routing(q, c):
                b = q * 4 + c
                pe.wait_ge(route_steps, FIRST + 3 * b + 3)
                nc.tensor.transpose(p_l[0:NE, P:2 * P], rt[:, :], ident[:, :]).then_inc(rt_turned, 1)

            def scales(q, c):
                b = q * 4 + c
                pe.wait_ge(rT_out, FIRST + b + 1)
                for k in range(KT):
                    mm = nc.tensor.matmul(p_t[:, k * P:(k + 1) * P], ics[:, k * P:(k + 1) * P], rT[:, :],
                                          start=True, stop=True)
                mm.then_inc(in_scaled, 1)
                pe.wait_ge(osc_out, FIRST + b)
                for h in range(2):
                    mm = nc.tensor.matmul(p_o[:, h * BANK:(h + 1) * BANK], rT[:, :], ocs[:, h * BANK:(h + 1) * BANK],
                                          start=True, stop=True)
                mm.then_inc(out_scaled, 1)

            def main(q, c, part):
                b = q * 4 + c
                if part == 0:
                    pe.wait_ge(xs_lo, FIRST + b + 1)
                    pe.wait_ge(y_done, FIRST + b)
                for k in range(2 * part, 2 * part + 2):
                    for h in range(2):
                        for n, t in enumerate(("hi", "lo")):
                            mm = nc.tensor.matmul(p_y[:, h * BANK:(h + 1) * BANK],
                                                  xs_part[t, c % 2][:, k * P:(k + 1) * P],
                                                  w[:, k, h * BANK:(h + 1) * BANK],
                                                  start=(k == 0 and n == 0), stop=(k == KT - 1 and n == 1))
                if part == 3:
                    mm.then_inc(main_done, 1)

            pe.wait_ge(const_pool, FIRST + 5)
            pe.wait_ge(const_in, 80)
            turn(0, 0)
            logits(0, 0)
            turn_routing(0, 0)
            scales(0, 0)
            pe.wait_ge(w_ready, FIRST + KT)

            def step(q, c, last):
                ahead = not (last and c == 3)
                if ahead:
                    turn(q, c + 1)
                main(q, c, 0)
                if ahead:
                    logits(q, c + 1)
                main(q, c, 1)
                if ahead:
                    turn_routing(q, c + 1)
                main(q, c, 2)
                if ahead:
                    scales(q, c + 1)
                main(q, c, 3)

            with pe.Fori(0, QUADS - 1) as q:
                for c in range(4):
                    step(q, c, False)
            for c in range(4):
                step(QUADS - 1, c, True)


def flamingo_layers(nc, a, out):
    def scratch(name, shape):
        return nc.dram_tensor(name, shape, F32, kind="Internal").ap()

    x2 = scratch("x_after_layer0", (BATCH, SEQ, DM))
    x3 = scratch("x_after_attention", (BATCH, SEQ, DM))
    xnT = scratch("xn_turned", (BATCH, P, KT, SEQ))
    ctxT = scratch("ctx_turned", (BATCH, P, KT, SEQ))
    linear_attention_moe_stage(nc, a["x"], a["ctx"], a["L0_WqT"], a["L0_WkT"], a["L0_Wv"], a["L0_WoT"], a["L0_bo"],
                               a["L0_g"], a["gate_x0"], a["gate_f0"], a["L0_WbT"], a["L0_bias"], a["L0_AT"],
                               a["L0_WrT"], a["L0_BmT"], a["prio"], x2, xnT, ctxT)
    gqa_stage(nc, x2, xnT, ctxT, a["mask"], a["gate_x1"], a["L1_Wq"], a["L1_Wk"], a["L1_Wv"], a["L1_Wo"],
              a["cos"], a["sin"], x3)
    sign_ffn_stage(nc, x3, a["gate_f1"], a["L1_signT"], a["L1_bias"], a["L1_gateT"], a["L1_in_scale"],
                   a["L1_out_scale"], out)


def rotary_tables(seq, d):
    inv_freq = (1.0 / 10000.0 ** (np.arange(0, d, 2, dtype=np.float32) / np.float32(d))).astype(np.float32)
    phase = inv_freq[:, None] * np.arange(seq, dtype=np.float32)[None, :]
    cos, sin = np.cos(phase), np.sin(phase)
    return np.concatenate([cos, cos]), np.concatenate([sin, -sin])


def kernel(**inputs):
    import concourse.bacc as _bacc
    from concourse.bass_utils import run_bass_kernel_spmd as _run

    v = {k: np.asarray(x) for k, x in inputs.items()}

    def rows(t):
        return np.broadcast_to(t.reshape(1, -1), (P, t.size))

    cos, sin = rotary_tables(SEQ, P)
    laid_out = {
        "x": v["x"], "ctx": v["ctx_4096"],
        "mask": v["mask_1x1xSxS2_bk0"].reshape(SEQ, SEQ).view(np.uint32),
        "gate_x0": rows(v["g_xattn"][0:1]), "gate_x1": rows(v["g_xattn"][1:2]),
        "gate_f0": rows(v["g_ffn"][0:1]), "gate_f1": rows(v["g_ffn"][1:2]),
        "L0_WqT": v["L0_xattn_Wq"].T, "L0_WkT": v["L0_xattn_Wk"].T, "L0_Wv": v["L0_xattn_Wv"],
        "L0_WoT": v["L0_xattn_Wo"].T, "L0_bo": v["L0_xattn_bo"].reshape(P, 1), "L0_g": v["L0_xattn_g"].reshape(P, 1),
        "L0_WbT": v["L0_ffn_Wb"].T, "L0_bias": rows(v["L0_ffn_bias"]),
        "L0_AT": v["L0_ffn_A"].reshape(-1, DM).T, "L0_WrT": v["L0_ffn_Wr"].T,
        "L0_BmT": v["L0_ffn_Bm"].transpose(0, 2, 1).reshape(-1, DM),
        "prio": rows(np.arange(8, 0, -1, dtype=np.float32)),
        "L1_Wq": v["L1_xattn_Wq"], "L1_Wk": v["L1_xattn_Wk"], "L1_Wv": v["L1_xattn_Wv"], "L1_Wo": v["L1_xattn_Wo"],
        "cos": cos, "sin": sin,
        "L1_signT": v["L1_ffn_weight"].T, "L1_bias": rows(v["L1_ffn_bias"]), "L1_gateT": v["L1_ffn_gate_w"].T,
        "L1_in_scale": v["L1_ffn_in_channel_scale"], "L1_out_scale": v["L1_ffn_out_channel_scale"],
    }
    nc = _bacc.Bacc("TRN2", target_bir_lowering=False, num_devices=1)
    arrays, args = {}, {}
    for name, a in laid_out.items():
        a = np.ascontiguousarray(a)
        arrays[f"in_{name}"] = a
        args[name] = nc.dram_tensor(f"in_{name}", a.shape, mybir.dt.from_np(a.dtype), kind="ExternalInput").ap()
    out = nc.dram_tensor("out_x", (BATCH, SEQ, DM), F32, kind="ExternalOutput").ap()
    flamingo_layers(nc, args, out)
    r = _run(nc, [arrays], core_ids=[0])
    return r.results[0]["out_x"]
```
